# Optimizing a Trainium2 kernel written in Bass

```python
import numpy as np
import jax
import jax.numpy as jnp

def _softmax(x, axis=-1):
    return jax.nn.softmax(x, axis=axis)

def _gelu(x):
    return jax.nn.gelu(x, approximate=True)

def _silu(x):
    return jax.nn.silu(x)

def _sigmoid(x):
    return jax.nn.sigmoid(x)

def _layernorm(x, axis=-1, eps=1e-05):
    m = jnp.mean(x, axis=axis, keepdims=True)
    v = jnp.var(x, axis=axis, keepdims=True)
    return (x - m) / jnp.sqrt(v + eps)

def _scatter_add(tgt, idx, src, axis=0):
    return tgt.at[idx].add(src)

def _segment_sum(src, seg, n):
    return jax.ops.segment_sum(src, seg, n)
kernel_name = 'mk_early_fusion_d1_tok_img768_r4_a5ba35'

def setup_inputs(seed: int=0):
    np.random.seed(seed)
    _w = jnp.asarray

    def _rec_inputs():
        import jax
        import jax.numpy as jnp
        _rk = jax.random.key(seed)
        x = -0.000147625 + 0.999875 * jax.random.normal(jax.random.fold_in(_rk, 1), (16, 12, 224, 224), jnp.float32)
        txt = -0.0221329 + 10 * jax.random.normal(jax.random.fold_in(_rk, 2), (16, 128, 192), jnp.float32)
        return (x, txt)
    x, txt = _rec_inputs()

    def _L0_tok_setup():
        import jax, jax.numpy as jnp
        import numpy as np
        IMG = 224
        PATCH = 16
        EMBED = 192
        C = 12
        B = 64
        key = jax.random.key(seed)
        k1, k2 = jax.random.split(key)
        x = jax.random.normal(k1, (B, C, IMG, IMG), dtype=jnp.float32)
        channel_weights = jax.random.normal(k2, (C, EMBED), dtype=jnp.float32)
        return {'x': x, 'channel_weights': channel_weights}
    _L0_tok_all = _L0_tok_setup()
    _L0_tok_in = {k: v for k, v in _L0_tok_all.items() if k in ('channel_weights',)}
    del _L0_tok_all

    def _L0_attn_setup():
        import jax, jax.numpy as jnp
        import numpy as np
        NUM_HEADS = 12
        WINDOW = 64
        LN_EPS = 1e-05

        def _ln(x, g, b):
            m = x.mean(-1, keepdims=True)
            v = x.var(-1, keepdims=True)
            return (x - m) / jnp.sqrt(v + LN_EPS) * g + b
        key = jax.random.key(seed)
        ks = jax.random.split(key, 10)
        B, L, D = (1, 512, 192)
        s = 0.02

        def w(k, shape):
            return jax.random.normal(k, shape, jnp.float32) * s
        return {'x': jax.random.normal(ks[0], (B, L, D), jnp.float32), 'ln1_g': jnp.ones((D,), jnp.float32), 'ln1_b': jnp.zeros((D,), jnp.float32), 'attn_qkv_w': w(ks[1], (D, 3 * D)), 'attn_qkv_b': jnp.zeros((3 * D,), jnp.float32), 'attn_proj_w': w(ks[2], (D, D)), 'attn_proj_b': jnp.zeros((D,), jnp.float32), 'ssm_qkv_w': w(ks[3], (D, 3 * D)), 'ssm_qkv_b': jnp.zeros((3 * D,), jnp.float32), 'ssm_out_w': w(ks[4], (D, D)), 'ssm_out_b': jnp.zeros((D,), jnp.float32), 'ssm_ln_g': jnp.ones((D,), jnp.float32), 'ssm_ln_b': jnp.zeros((D,), jnp.float32), 'out_w': w(ks[5], (D, D)), 'out_b': jnp.zeros((D,), jnp.float32), 'mlp_w1': w(ks[6], (D, 4 * D)), 'mlp_b1': jnp.zeros((4 * D,), jnp.float32), 'mlp_w2': w(ks[7], (4 * D, D)), 'mlp_b2': jnp.zeros((D,), jnp.float32), 'lnm_g': jnp.ones((D,), jnp.float32), 'lnm_b': jnp.zeros((D,), jnp.float32)}
    _L0_attn_all = _L0_attn_setup()
    _L0_attn_in = {k: v for k, v in _L0_attn_all.items() if k in ('ln1_g', 'ln1_b', 'attn_qkv_w', 'attn_qkv_b', 'attn_proj_w', 'attn_proj_b', 'ssm_qkv_w', 'ssm_qkv_b', 'ssm_out_w', 'ssm_out_b', 'ssm_ln_g', 'ssm_ln_b', 'out_w', 'out_b', 'mlp_w1', 'mlp_b1', 'mlp_w2', 'mlp_b2', 'lnm_g', 'lnm_b')}
    del _L0_attn_all

    def _L0_ffn_setup():
        import jax, jax.numpy as jnp
        import numpy as np
        DIM = 192
        NUM_EXPERTS = 8
        HIDDEN = 768
        TOP_K = 2
        B, N = (1, 256)
        key = jax.random.key(seed)
        ks = jax.random.split(key, 8)
        s_in = 1.0 / np.sqrt(DIM)
        s_hid = 1.0 / np.sqrt(HIDDEN)
        return {'x': jax.random.normal(ks[0], (B, N, DIM), dtype=jnp.float32), 'Wg': jax.random.uniform(ks[1], (DIM, NUM_EXPERTS), jnp.float32, -s_in, s_in), 'bg': jax.random.uniform(ks[2], (NUM_EXPERTS,), jnp.float32, -s_in, s_in), 'W1': jax.random.uniform(ks[3], (NUM_EXPERTS, DIM, HIDDEN), jnp.float32, -s_in, s_in), 'b1': jax.random.uniform(ks[4], (NUM_EXPERTS, HIDDEN), jnp.float32, -s_in, s_in), 'W2': jax.random.uniform(ks[5], (NUM_EXPERTS, HIDDEN, DIM), jnp.float32, -s_hid, s_hid), 'b2': jax.random.uniform(ks[6], (NUM_EXPERTS, DIM), jnp.float32, -s_hid, s_hid)}
    _L0_ffn_all = _L0_ffn_setup()
    _L0_ffn_in = {k: v for k, v in _L0_ffn_all.items() if k in ('Wg', 'bg', 'W1', 'b1', 'W2', 'b2')}
    del _L0_ffn_all
    return {'x': x, 'txt': txt, 'L0_tok_channel_weights': _L0_tok_in['channel_weights'], 'L0_attn_ln1_g': _L0_attn_in['ln1_g'], 'L0_attn_ln1_b': _L0_attn_in['ln1_b'], 'L0_attn_attn_qkv_w': _L0_attn_in['attn_qkv_w'], 'L0_attn_attn_qkv_b': _L0_attn_in['attn_qkv_b'], 'L0_attn_attn_proj_w': _L0_attn_in['attn_proj_w'], 'L0_attn_attn_proj_b': _L0_attn_in['attn_proj_b'], 'L0_attn_ssm_qkv_w': _L0_attn_in['ssm_qkv_w'], 'L0_attn_ssm_qkv_b': _L0_attn_in['ssm_qkv_b'], 'L0_attn_ssm_out_w': _L0_attn_in['ssm_out_w'], 'L0_attn_ssm_out_b': _L0_attn_in['ssm_out_b'], 'L0_attn_ssm_ln_g': _L0_attn_in['ssm_ln_g'], 'L0_attn_ssm_ln_b': _L0_attn_in['ssm_ln_b'], 'L0_attn_out_w': _L0_attn_in['out_w'], 'L0_attn_out_b': _L0_attn_in['out_b'], 'L0_attn_mlp_w1': _L0_attn_in['mlp_w1'], 'L0_attn_mlp_b1': _L0_attn_in['mlp_b1'], 'L0_attn_mlp_w2': _L0_attn_in['mlp_w2'], 'L0_attn_mlp_b2': _L0_attn_in['mlp_b2'], 'L0_attn_lnm_g': _L0_attn_in['lnm_g'], 'L0_attn_lnm_b': _L0_attn_in['lnm_b'], 'L0_ffn_Wg': _L0_ffn_in['Wg'], 'L0_ffn_bg': _L0_ffn_in['bg'], 'L0_ffn_W1': _L0_ffn_in['W1'], 'L0_ffn_b1': _L0_ffn_in['b1'], 'L0_ffn_W2': _L0_ffn_in['W2'], 'L0_ffn_b2': _L0_ffn_in['b2']}

def reference(x, txt, L0_tok_channel_weights, L0_attn_ln1_g, L0_attn_ln1_b, L0_attn_attn_qkv_w, L0_attn_attn_qkv_b, L0_attn_attn_proj_w, L0_attn_attn_proj_b, L0_attn_ssm_qkv_w, L0_attn_ssm_qkv_b, L0_attn_ssm_out_w, L0_attn_ssm_out_b, L0_attn_ssm_ln_g, L0_attn_ssm_ln_b, L0_attn_out_w, L0_attn_out_b, L0_attn_mlp_w1, L0_attn_mlp_b1, L0_attn_mlp_w2, L0_attn_mlp_b2, L0_attn_lnm_g, L0_attn_lnm_b, L0_ffn_Wg, L0_ffn_bg, L0_ffn_W1, L0_ffn_b1, L0_ffn_W2, L0_ffn_b2):
    import jax
    import jax.numpy as jnp

    def _L0_tok_ref(x, channel_weights):
        import jax, jax.numpy as jnp
        import numpy as np
        IMG = 224
        PATCH = 16
        EMBED = 192
        C = 12
        B = 64
        Bb, Cc, H, W = x.shape
        K = PATCH
        n = H // K
        pooled = x.reshape(Bb, Cc, n, K, n, K).sum(axis=(3, 5))
        out = jnp.einsum('bcij,ce->bije', pooled, channel_weights)
        return out.reshape(Bb, n * n, EMBED)

    def _L0_attn_ref(x, ln1_g, ln1_b, attn_qkv_w, attn_qkv_b, attn_proj_w, attn_proj_b, ssm_qkv_w, ssm_qkv_b, ssm_out_w, ssm_out_b, ssm_ln_g, ssm_ln_b, out_w, out_b, mlp_w1, mlp_b1, mlp_w2, mlp_b2, lnm_g, lnm_b):
        import jax, jax.numpy as jnp
        import numpy as np
        NUM_HEADS = 12
        WINDOW = 64
        LN_EPS = 1e-05

        def _ln(x, g, b):
            m = x.mean(-1, keepdims=True)
            v = x.var(-1, keepdims=True)
            return (x - m) / jnp.sqrt(v + LN_EPS) * g + b
        B, L, D = x.shape
        H = NUM_HEADS
        E = D // H
        xn = _ln(x, ln1_g, ln1_b)
        qkv = (xn @ attn_qkv_w + attn_qkv_b).reshape(B, L, 3, H, E)
        q = jnp.transpose(qkv[:, :, 0], (0, 2, 1, 3))
        k = jnp.transpose(qkv[:, :, 1], (0, 2, 1, 3))
        v = jnp.transpose(qkv[:, :, 2], (0, 2, 1, 3))
        scale = 1.0 / jnp.sqrt(jnp.float32(E))
        scores = jnp.einsum('bhqe,bhke->bhqk', q, k) * scale
        i = jnp.arange(L)[:, None]
        j = jnp.arange(L)[None, :]
        mask = (j > i) | (j <= i - WINDOW)
        scores = jnp.where(mask, jnp.float32(-10000.0), scores)
        attn = jax.nn.softmax(scores, axis=-1)
        ao = jnp.einsum('bhqk,bhke->bhqe', attn, v)
        ao = jnp.transpose(ao, (0, 2, 1, 3)).reshape(B, L, D)
        ao = ao @ attn_proj_w + attn_proj_b
        qkv2 = xn @ ssm_qkv_w + ssm_qkv_b
        q2, k2, v2 = jnp.split(qkv2, 3, axis=-1)
        q2 = q2.reshape(B, L, H, E)
        k2 = k2.reshape(B, L, H, E)
        v2 = v2.reshape(B, L, H, E)
        q2 = jax.nn.elu(q2) + (1.0 + 0.0001)
        k2 = jax.nn.elu(k2) + (1.0 + 0.0001)
        q2 = q2 * scale
        kv = jnp.einsum('blhe,blhf->blhef', k2, v2)
        kv_cumsum = jnp.cumsum(kv, axis=1)
        k_cumsum = jnp.cumsum(k2, axis=1)
        num = jnp.einsum('blhe,blhef->blhf', q2, kv_cumsum)
        den = jnp.einsum('blhe,blhe->blh', q2, k_cumsum)[..., None] + 0.0001
        so = (num / den).reshape(B, L, D)
        so = so @ ssm_out_w + ssm_out_b
        so = _ln(so, ssm_ln_g, ssm_ln_b)
        x2 = x + (ao + so) @ out_w + out_b
        h = _ln(x2, lnm_g, lnm_b)
        h = jax.nn.gelu(h @ mlp_w1 + mlp_b1, approximate=False)
        return x2 + (h @ mlp_w2 + mlp_b2)

    def _L0_ffn_ref(x, Wg, bg, W1, b1, W2, b2):
        import jax, jax.numpy as jnp
        import numpy as np
        DIM = 192
        NUM_EXPERTS = 8
        HIDDEN = 768
        TOP_K = 2
        B, N = (1, 256)
        Bc, Nc, D = x.shape
        xt = x.reshape(-1, D)
        gate = xt @ Wg + bg
        scores, idx = jax.lax.top_k(gate, TOP_K)
        h = jax.nn.gelu(jnp.einsum('td,edh->eth', xt, W1) + b1[:, None, :], approximate=False)
        y = jnp.einsum('eth,ehd->etd', h, W2) + b2[:, None, :]
        comb = jnp.sum(jax.nn.one_hot(idx, NUM_EXPERTS, dtype=x.dtype) * scores[..., None], axis=1)
        out = jnp.einsum('te,etd->td', comb, y)
        return out.reshape(Bc, Nc, D)
    h = _L0_tok_ref(x, L0_tok_channel_weights)
    h = jnp.concatenate([h, txt], axis=1)
    h = h + _L0_attn_ref(_layernorm(h, axis=-1), L0_attn_ln1_g, L0_attn_ln1_b, L0_attn_attn_qkv_w, L0_attn_attn_qkv_b, L0_attn_attn_proj_w, L0_attn_attn_proj_b, L0_attn_ssm_qkv_w, L0_attn_ssm_qkv_b, L0_attn_ssm_out_w, L0_attn_ssm_out_b, L0_attn_ssm_ln_g, L0_attn_ssm_ln_b, L0_attn_out_w, L0_attn_out_b, L0_attn_mlp_w1, L0_attn_mlp_b1, L0_attn_mlp_w2, L0_attn_mlp_b2, L0_attn_lnm_g, L0_attn_lnm_b)
    h = h + _L0_ffn_ref(_layernorm(h, axis=-1), L0_ffn_Wg, L0_ffn_bg, L0_ffn_W1, L0_ffn_b1, L0_ffn_W2, L0_ffn_b2)
    return h

_drawn_inputs = setup_inputs


def setup_inputs(seed=0):
    import zlib

    import numpy as np

    out = dict(_drawn_inputs(seed))
    spreads = {'L0_attn_ln1_g': (1.0, 0.6),
     'L0_attn_ln1_b': (0.0, 0.8),
     'L0_attn_attn_qkv_b': (0.0, 0.8),
     'L0_attn_attn_proj_b': (0.0, 0.8),
     'L0_attn_ssm_qkv_b': (0.0, 0.8),
     'L0_attn_ssm_out_b': (0.0, 0.8),
     'L0_attn_ssm_ln_g': (1.0, 0.6),
     'L0_attn_ssm_ln_b': (0.0, 0.8),
     'L0_attn_out_b': (0.0, 0.8),
     'L0_attn_mlp_b1': (0.0, 0.8),
     'L0_attn_mlp_b2': (0.0, 0.8),
     'L0_attn_lnm_g': (1.0, 0.6),
     'L0_attn_lnm_b': (0.0, 0.8)}
    factors = {'L0_attn_attn_qkv_w': 8.0,
     'L0_attn_attn_proj_w': 8.0,
     'L0_attn_ssm_qkv_w': 8.0,
     'L0_attn_ssm_out_w': 8.0,
     'L0_attn_out_w': 8.0,
     'L0_attn_mlp_w1': 8.0,
     'L0_attn_mlp_w2': 8.0,
     'L0_ffn_Wg': 8.0,
     'L0_ffn_bg': 8.0,
     'L0_ffn_W1': 8.0,
     'L0_ffn_b1': 8.0,
     'L0_ffn_W2': 8.0,
     'L0_ffn_b2': 43.789}
    for name, (base, spread) in spreads.items():
        noise = np.random.default_rng([zlib.crc32(name.encode()), seed]).standard_normal(out[name].shape)
        drawn = base * np.exp(spread * noise) if base else spread * noise
        out[name] = jnp.asarray(drawn.astype(out[name].dtype))
    for name, factor in factors.items():
        out[name] = (out[name] * factor).astype(out[name].dtype)
    return out
```

```python
import concourse.bass as bass
from concourse import mybir
from contextlib import ExitStack


def early_fusion_moe_kernel(nc, x, txt, cw, ln1_g, ln1_b, qkv_w, qkv_b, proj_w, proj_b,
                            sqkv_w, sqkv_b, sout_w, sout_b, sln_g, sln_b, out_w, out_b,
                            mlp_w1, mlp_b1, mlp_w2, mlp_b2, lnm_g, lnm_b,
                            Wg, bg, W1, b1, W2, b2, out):
    fp32 = mybir.dt.float32
    bf16 = mybir.dt.bfloat16
    u32 = mybir.dt.uint32
    ALU = mybir.AluOpType
    ACT = mybir.ActivationFunctionType
    AX = mybir.AxisListType

    S, C, IMG, _ = x.shape
    D = cw.shape[1]
    KP = 16
    NP = IMG // KP
    IT = NP * NP
    TX = txt.shape[1]
    L = IT + TX
    T = 3
    P = L // T
    I1 = IT - P
    H = 12
    E = D // H
    HC = H // 2
    NU = H // 2
    WIN = 64
    W = P + WIN - 1
    DC = D // 2
    HID = mlp_w1.shape[1]
    NJ = HID // 128
    NE = Wg.shape[1]
    GC = C // 3
    PX = GC * NP * 2
    RW = IMG * KP // 2
    EPS = 1e-5
    FAR = -1e9

    ctx = ExitStack()
    with ctx:
        def sb(name, shape, dt=fp32):
            return ctx.enter_context(nc.sbuf_tensor(name, shape, dt))

        def sem(name):
            return ctx.enter_context(nc.semaphore(name))

        cwrep = sb("cwrep", [PX, 3, D])
        wqk = sb("wqk", [DC + 1, 2, 4, D])
        wv = sb("wv", [DC + 1, 2, 2, D])
        wproj = sb("wproj", [DC + 1, 2, D])
        wsout = sb("wsout", [DC + 1, 2, D])
        wout = sb("wout", [DC + 1, 2, D])
        wm1 = sb("wm1", [DC + 1, 2, HID])
        wm2 = sb("wm2", [128, NJ, D])
        bm2 = sb("bm2", [1, D])
        wg = sb("wg", [DC + 1, 2, NE])
        w1 = sb("w1", [DC + 1, 2, NE, HID])
        w2 = sb("w2", [128, NE, NJ, D])
        b2s = sb("b2s", [NE, D])
        lnw = sb("lnw", [P, 3, 2, D])
        ident = sb("ident", [128, 128])
        identb = sb("identb", [128, 128], bf16)
        band = sb("band", [P, W], bf16)
        causal = sb("causal", [P, L])
        headm = sb("headm", [DC, HC])
        patchm = sb("patchm", [PX, NP])
        iota8 = sb("iota8", [P, NE])
        mhalf = sb("mhalf", [P, T])

        xin = sb("xin", [PX, 2, RW])
        pooled = sb("pooled", [PX, 3, NP])
        patch = sb("patch", [PX, 3, NP, NP])
        h0 = sb("h0", [P, T, D])
        y = sb("y", [P, T, D])
        xn = sb("xn", [P, T, D])
        stats = sb("stats", [P, T, 6])
        mv = sb("mv", [P, T, 2])
        rstd = sb("rstd", [P, T])
        tA = sb("tA", [DC + 1, 2, L])
        tB = sb("tB", [DC + 1, 2, L])
        zT = sb("zT", [DC + 1, 2, L])
        qT = sb("qT", [DC, 2, L])
        kT = sb("kT", [DC, 2, L])
        sqT = sb("sqT", [DC, 2, L])
        skT = sb("skT", [DC, 2, L])
        NX = 3
        hX = sb("hX", [DC, NX, 2, L])
        elue = sb("elue", [DC, L])
        elur = sb("elur", [DC, L])
        va = sb("va", [P, T, H, E + 1])
        vs = sb("vs", [P, T, H, E + 1])
        nmax = sb("nmax", [P, 2, 2])
        prob = sb("prob", [P, 2, 2, 2 * P])
        probT = sb("probT", [P, 2, 2, 2, P])
        att = [sb(f"att{kt}", [P, 2, L - kt * P]) for kt in range(T)]
        den = sb("den", [P, T, 2])
        ao = sb("ao", [P, T, H, E])
        so = sb("so", [P, T, H, E])
        so2 = sb("so2", [P, T, D])
        NH_ = 3
        hmT = sb("hmT", [128, NH_, L])
        hT = sb("hT", [128, NH_, L])
        hres = sb("hres", [P, T, D])
        gate = sb("gate", [P, T, NE])
        top8 = sb("top8", [P, T, 8])
        idx8 = sb("idx8", [P, T, 8], u32)
        idxf = sb("idxf", [P, T, 8])
        comb = sb("comb", [P, T, NE])
        comb2 = sb("comb2", [P, T, NE])
        combT = sb("combT", [NE, L])

        bank = [ctx.enter_context(nc.psum_tensor(f"bank{i}", [128, 512], fp32)) for i in range(8)]

        ring_a, acc_a, ring_h, ring_y = (0, 1, 2), 7, (3, 4), (5, 6)
        PAIRS = ((0, 2), (2, 3))
        UNITS = [(u, t) for u in range(NU) for t in range(T)]
        SC = [(0, 0, 1), (0, 1, 1), (1, 0, 2), (2, 0, 2)]
        place, turn = {}, [0] * 8

        def plan(name, b):
            place[name] = (b, turn[b])
            turn[b] += 1

        ring = [0]

        def plan_a(name):
            plan(name, ring_a[ring[0] % 3])
            ring[0] += 1

        for t in range(2):
            plan_a(("tok", t))
        for c in range(2):
            plan_a(("xnT", c))
        for m in range(8):
            plan_a(("qk", m))
        for t in range(T):
            plan_a(("v", t))
        for u in range(NU):
            plan(("ao", u), acc_a)
        for k in range(len(UNITS) + 1):
            if k < len(UNITS):
                plan_a(("score", k))
            if k > 0:
                plan_a(("probT", k - 1))
        for u in range(NU):
            for s in range(len(SC)):
                plan_a(("ssm", u, s))
            plan(("so", u), acc_a)
        for name in ("soT", "so2", "aoT", "sum", "smT", "out", "x2T"):
            for c in range(2):
                plan_a((name, c))
        for j in range(NJ):
            plan(("mh", j), ring_a[j % 2])
        plan(("my", 0), acc_a)
        plan(("my", 1), ring_a[2])
        for name in (("zT", 0), ("zT", 1), ("gate",), ("combT",)):
            plan_a(name)
        for pair in range(2):
            plan(("cb", pair), ring_y[pair])
        for e in range(NE):
            for j in range(NJ):
                plan(("hid", e, j), ring_h[j % 2])
            for pair in range(2):
                plan(("ye", e, pair), ring_y[pair])

        class Count:
            def __init__(self, name, per):
                self.sem, self.per = sem(name), per
                counts.append(self)

            def now(self, n, k):
                return n * self.per + (self.per + k)

            def before(self, n, k):
                return n * self.per + k

        counts = []
        full = [Count(f"bank{b}_full", turn[b]) for b in range(8)]
        read = [Count(f"bank{b}_read", turn[b]) for b in range(8)]

        def wait_full(eng, n, name):
            b, k = place[name]
            eng.wait_ge(full[b].sem, full[b].now(n, k + 1))

        def wait_read(eng, n, name):
            b, k = place[name]
            eng.wait_ge(read[b].sem, read[b].now(n, k + 1))

        def wait_free(eng, n, name):
            b, k = place[name]
            eng.wait_ge(read[b].sem, read[b].now(n, k) if k else read[b].before(n, turn[b]))

        def at(name):
            return bank[place[name][0]]

        def fullsem(name):
            return full[place[name][0]].sem

        def readsem(name):
            return read[place[name][0]].sem

        ORDER = [("front", None), ("experts", 0), ("qk", None), ("experts", 1), ("attention", 0), ("attention", 1),
                 ("experts", 2), ("attention", 2), ("attention", 3), ("experts", 3), ("attention", 4), ("attention", 5),
                 ("experts", 4), ("ssm", 0), ("ssm", 1), ("experts", 5), ("ssm", 2), ("ssm", 3), ("experts", 6),
                 ("ssm", 4), ("ssm", 5), ("experts", 7), ("tail", None), ("experts", 8), ("mlp", None)]
        NWA, NWB, NSETUP, VLINKS = 53, 12, 28, 41

        def run_schedule(stage, eng, first_experts=None):
            def body(n, m):
                for name, k in ORDER:
                    at_sample = m if name == "experts" else n
                    if at_sample is None:
                        continue
                    if k is None:
                        stage[name](at_sample)
                    else:
                        stage[name](at_sample, k)

            body(0, None)
            if first_experts:
                first_experts()
            with eng.Fori(1, S) as i:
                body(i, i - 1)
            body(None, S - 1)

        setup = sem("setup")
        weights_a = sem("weights_a")
        weights_b = sem("weights_b")
        x_loaded = [Count(f"x_loaded{g}", 16) for g in range(3)]
        x_read = Count("x_read", 3)
        txt_loaded = Count("txt_loaded", 32)
        h0_done = Count("h0_done", 1)
        patch_ready = Count("patch_ready", 3)
        var_ready = Count("var_ready", 5)
        eps_added = Count("eps_added", 5)
        rstd_ready = Count("rstd_ready", 5)
        xn_ready = Count("xn_ready", 1)
        elu_exp = Count("elu_exp", 4)
        elu_ready = Count("elu_ready", 4)
        hX_ready = Count("hX_ready", 2 * NU)
        nmax_ready = Count("nmax_ready", len(UNITS))
        x2n_ready = Count("x2n_ready", 1)
        z_ready = Count("z_ready", 1)
        comb_ready = Count("comb_ready", 1)
        stored = Count("stored", 16)
        linked = Count("linked", VLINKS)

        held = sem("held")

        def hold(eng):
            eng.sem_inc(held, 1)

        block = ctx.enter_context(nc.Block())

        @block.sync
        def _(sp):
            def load(dst, src, s):
                sp.dma_start(dst, src).then_inc(s, 16)
                return 1

            n = 0
            for c in range(2):
                r = slice(c * DC, (c + 1) * DC)
                for k, (w, m) in enumerate(((qkv_w, 0), (qkv_w, 1), (sqkv_w, 0), (sqkv_w, 1))):
                    n += load(wqk[0:DC, c, k, :], w[r, m * D:(m + 1) * D], weights_a)
                n += load(wv[0:DC, c, 0, :], qkv_w[r, 2 * D:3 * D], weights_a)
                n += load(wv[0:DC, c, 1, :], sqkv_w[r, 2 * D:3 * D], weights_a)
                for dst, w in ((wproj, proj_w), (wsout, sout_w), (wout, out_w), (wm1, mlp_w1), (wg, Wg)):
                    n += load(dst[0:DC, c, :], w[r, :], weights_a)
            for k, (w, m) in enumerate(((qkv_b, 0), (qkv_b, 1), (sqkv_b, 0), (sqkv_b, 1))):
                n += load(wqk[DC:DC + 1, 1, k, :], w[m * D:(m + 1) * D].rearrange("(o d) -> o d", o=1), weights_a)
            n += load(wv[DC:DC + 1, 1, 0, :], qkv_b[2 * D:3 * D].rearrange("(o d) -> o d", o=1), weights_a)
            n += load(wv[DC:DC + 1, 1, 1, :], sqkv_b[2 * D:3 * D].rearrange("(o d) -> o d", o=1), weights_a)
            for dst, b in ((wproj, proj_b), (wsout, sout_b), (wout, out_b), (wm1, mlp_b1), (wg, bg)):
                n += load(dst[DC:DC + 1, 1, :], b.rearrange("(o d) -> o d", o=1), weights_a)
            n += load(wm2[:, :, :], mlp_w2.rearrange("(j p) d -> p j d", p=128), weights_a)
            n += load(bm2[:, :], mlp_b2.rearrange("(o d) -> o d", o=1), weights_a)
            for g in range(3):
                for c in range(GC):
                    n += load(cwrep[c * 2 * NP:(c + 1) * 2 * NP, g, :],
                              cw[g * GC + c:g * GC + c + 1, :].to_broadcast((2 * NP, D)), weights_a)
            for k, (g_, b_) in enumerate(((ln1_g, ln1_b), (sln_g, sln_b), (lnm_g, lnm_b))):
                n += load(lnw[:, k, 0, :], g_.rearrange("(o d) -> o d", o=1).to_broadcast((P, D)), weights_a)
                n += load(lnw[:, k, 1, :], b_.rearrange("(o d) -> o d", o=1).to_broadcast((P, D)), weights_a)
            assert n == NWA, n
            n = 0
            for c in range(2):
                n += load(w1[0:DC, c, :, :], W1[:, c * DC:(c + 1) * DC, :].rearrange("e p f -> p e f"), weights_b)
            n += load(w1[DC:DC + 1, 1, :, :], b1.rearrange("(o e) f -> o e f", o=1), weights_b)
            for e in range(NE):
                n += load(w2[:, e, :, :], W2[e].rearrange("(j p) d -> p j d", p=128), weights_b)
            n += load(b2s[:, :], b2, weights_b)
            assert n == NWB, n

            x_v = x.rearrange("s (g c) (i b r) w -> s g (c i b) (r w)", g=3, i=NP, b=2)

            def load_sample(n, lead):
                for g in range(3):
                    sp.wait_ge(x_read.sem, lead[g])
                    sp.dma_start(xin[:, g % 2, :], x_v[bass.ds(n, 1), g, :, :].rearrange("s p f -> (s p) f")).then_inc(x_loaded[g].sem, 16)
                sp.wait_ge(h0_done.sem, lead[3])
                sp.dma_start(h0[I1:P, 1, :], txt[bass.ds(n, 1), 0:P - I1, :].rearrange("s p d -> (s p) d")).then_inc(txt_loaded.sem, 16)
                sp.dma_start(h0[:, 2, :], txt[bass.ds(n, 1), P - I1:TX, :].rearrange("s p d -> (s p) d")).then_inc(txt_loaded.sem, 16)

            def store_sample(n, lead):
                for b, v in zip(ring_y, lead):
                    sp.wait_ge(read[b].sem, v)
                sp.dma_start(out[bass.ds(n, 1), :, :].rearrange("s (t p) d -> p (s t) d", t=T), hres[:, :, :]).then_inc(stored.sem, 16)

            def leads(n):
                return [x_read.before(n, 3), x_read.before(n, 2), x_read.now(n, 1)] + [h0_done.before(n, 1)]

            load_sample(0, leads(0))
            with sp.Fori(1, S) as i:
                load_sample(i, [sp.snap(v) for v in leads(i)])
                store_sample(i - 1, [sp.snap(read[b].now(i - 1, turn[b])) for b in ring_y])
            store_sample(S - 1, [read[b].now(S - 1, turn[b]) for b in ring_y])
            sp.wait_ge(stored.sem, stored.now(S - 1, 16))

        @block.gpsimd
        def _(pool):
            steps = [0]

            def step(ins):
                steps[0] += 1
                ins.then_inc(setup, 1)
                pool.wait_ge(setup, steps[0])

            for c in counts:
                pool.sem_inc(c.sem, c.per)
            step(pool.memset(ident[:, :], 0.0))
            step(pool.memset(band[:, :], 0.0))
            step(pool.memset(causal[:, :], 1.0))
            step(pool.memset(headm[:, :], 1.0))
            step(pool.memset(mhalf[:, :], -0.5))
            step(pool.memset(prob[:, :, :, :], 0.0))
            step(pool.memset(va[:, :, :, :], 1.0))
            step(pool.memset(vs[:, :, :, :], 1.0))
            for b in (tA, tB, zT):
                step(pool.memset(b[DC:DC + 1, 1, :], 1.0))
            step(pool.iota(iota8[:, :], pattern=[[1, NE]], base=0, channel_multiplier=0, allow_small_or_imprecise_dtypes=True))
            step(pool.affine_select(out=ident[:, :], in_=ident[:, :], compare_op=ALU.not_equal, fill=1.0,
                                    base=0, pattern=[[-1, 128]], channel_multiplier=1))
            step(pool.affine_select(out=band[:, :], in_=band[:, :], compare_op=ALU.is_ge, fill=FAR,
                                    base=0, pattern=[[1, W]], channel_multiplier=-1))
            step(pool.affine_select(out=causal[:, :], in_=causal[:, :], compare_op=ALU.is_ge, fill=0.0,
                                    base=0, pattern=[[1, L]], channel_multiplier=-1))
            step(pool.affine_select(out=headm[:, :], in_=headm[:, :], compare_op=ALU.is_ge, fill=0.0,
                                    base=0, pattern=[[-E, HC]], channel_multiplier=1))
            step(pool.affine_select(out=band[:, :], in_=band[:, :], compare_op=ALU.is_ge, fill=FAR,
                                    base=WIN - 1, pattern=[[-1, W]], channel_multiplier=1))
            step(pool.affine_select(out=headm[:, :], in_=headm[:, :], compare_op=ALU.is_ge, fill=0.0,
                                    base=E - 1, pattern=[[E, HC]], channel_multiplier=-1))
            step(pool.tensor_copy(identb[:, :], ident[:, :]))
            step(pool.memset(patchm[:, :], 0.0))
            for c in range(GC):
                for b in range(2):
                    step(pool.affine_select(out=patchm[:, :], in_=patchm[:, :], compare_op=ALU.not_equal, fill=1.0,
                                            base=-(2 * NP * c + b), pattern=[[-2, NP]], channel_multiplier=1))
            assert steps[0] == NSETUP, steps[0]

            def deviation(n, k):
                pool.wait_ge(var_ready.sem, var_ready.now(n, k + 1))
                hold(pool)
                pool.tensor_scalar(rstd[:, :], mv[:, :, 1], EPS, None, ALU.add).then_inc(eps_added.sem, 1)
                pool.wait_ge(eps_added.sem, eps_added.now(n, k + 1))
                pool.tensor_tensor(rstd[:, :], rstd[:, :], mhalf[:, :], ALU.pow).then_inc(rstd_ready.sem, 1)

            def front(n):
                deviation(n, 0)
                deviation(n, 1)

            def copies(n, k, src):
                u = k % NU
                if k < NX:
                    pool.wait_ge(full[place[last_reader(k - NX + 2 * NU)][0]].sem,
                                 full[place[last_reader(k - NX + 2 * NU)][0]].before(n, place[last_reader(k - NX + 2 * NU)][1] + 1))
                else:
                    wait_full(pool, n, last_reader(k - NX))
                hold(pool)
                for i in range(2):
                    h = (2 * u + i) % HC
                    ins = pool.tensor_scalar(hX[:, k % NX, i, :], src[:, u // (NU // 2), :], headm[:, h:h + 1], None, ALU.mult)
                ins.then_inc(hX_ready.sem, 1)

            def last_reader(k):
                return ("score", T * k + T - 1) if k < NU else ("ssm", k - NU, len(SC) - 1)

            def sample(n):
                deviation(n, 0)
                deviation(n, 1)
                for u in range(NU):
                    if u % (NU // 2) == 0:
                        wait_read(pool, n, ("qk", 2 + u // (NU // 2)))
                    copies(n, u, kT)
                for u in range(NU):
                    if u % (NU // 2) == 0:
                        pool.wait_ge(elu_ready.sem, elu_ready.now(n, 1 + u // (NU // 2)))
                    copies(n, NU + u, sqT)
                for k in (2, 3, 4):
                    deviation(n, k)

            with pool.Fori(0, S) as n:
                sample(n)

        @block.tensor
        def _(pe):
            mm = nc.tensor.matmul

            def open_tile(n, name):
                wait_free(pe, n, name)
                return at(name)

            def transpose_tiles(n, name, src, c):
                o = open_tile(n, (name, c))
                for t in range(T):
                    ins = nc.tensor.transpose(o[0:DC, t * P:(t + 1) * P], src[:, t, c * DC:(c + 1) * DC], ident[0:P, 0:P])
                ins.then_inc(fullsem((name, c)), 1)

            def linear(n, name, xT, w, pair):
                o = open_tile(n, (name, pair))
                t0, t1 = PAIRS[pair]
                for t in range(t0, t1):
                    for c in range(2):
                        ins = mm(o[0:P, (t - t0) * D:(t - t0 + 1) * D], xT[0:DC + c, c, t * P:(t + 1) * P],
                                 w[0:DC + c, c, :], start=(c == 0), stop=(c == 1))
                ins.then_inc(fullsem((name, pair)), 1)

            def chunks(t):
                return (1,) if t == 0 else (0, 1)

            def front(n):
                pe.wait_ge(patch_ready.sem, patch_ready.now(n, 3))
                for t, (a, b) in enumerate(((0, P), (P, IT))):
                    o = open_tile(n, ("tok", t))
                    for g in range(3):
                        ins = mm(o[0:b - a, 0:D], patch[:, g, :, :].rearrange("p i j -> p (i j)")[:, a:b],
                                 cwrep[:, g, :], start=(g == 0), stop=(g == 2))
                    ins.then_inc(fullsem(("tok", t)), 1)
                pe.wait_ge(xn_ready.sem, xn_ready.now(n, 1))
                for c in range(2):
                    transpose_tiles(n, "xnT", xn, c)

            def qk(n):
                for c in range(2):
                    wait_read(pe, n, ("xnT", c))
                for m in range(8):
                    o = open_tile(n, ("qk", m))
                    for c in range(2):
                        ins = mm(o[0:DC, 0:L], wqk[0:DC + c, c, m // 2, (m % 2) * DC:(m % 2 + 1) * DC],
                                 tA[0:DC + c, c, :], start=(c == 0), stop=(c == 1))
                    ins.then_inc(fullsem(("qk", m)), 1)
                for t in range(T):
                    o = open_tile(n, ("v", t))
                    for c in range(2):
                        ins = mm(o[0:P, 0:2 * D], tA[0:DC + c, c, t * P:(t + 1) * P], wv[0:DC + c, c, :, :],
                                 start=(c == 0), stop=(c == 1))
                    ins.then_inc(fullsem(("v", t)), 1)

            def scores(n, k):
                u, t = UNITS[k]
                c = u // (NU // 2)
                if t == 0:
                    pe.wait_ge(hX_ready.sem, hX_ready.now(n, u + 1))
                if k == 0:
                    for c_ in range(2):
                        wait_read(pe, n, ("qk", c_))
                o = open_tile(n, ("score", k))
                w = P if t == 0 else W
                o = o[0:P, 0:2 * w].rearrange("p (i k) -> p i k", i=2)
                mm(o, identb[0:P, 0:P], band[:, None, W - w:W].to_broadcast((P, 2, w)), start=True, stop=False)
                mm(o, qT[:, c, t * P:(t + 1) * P], hX[:, u % NX, :, (t + 1) * P - w:(t + 1) * P],
                   start=False, stop=True).then_inc(fullsem(("score", k)), 1)

            def transposes(n, k):
                _, t = UNITS[k]
                wait_read(pe, n, ("score", k))
                o = open_tile(n, ("probT", k))[0:P, 0:4 * P].rearrange("p (i c q) -> p i c q", i=2, c=2)
                for i in range(2):
                    for c in chunks(t):
                        ins = nc.tensor.transpose(o[:, i, c, :], prob[:, k % 2, i, c * P:(c + 1) * P], ident[0:P, 0:P])
                ins.then_inc(fullsem(("probT", k)), 1)

            def values(n, k):
                u, t = UNITS[k]
                if k == 0:
                    for t_ in range(T):
                        wait_read(pe, n, ("v", t_))
                if t == 0:
                    open_tile(n, ("ao", u))
                wait_read(pe, n, ("probT", k))
                o = at(("ao", u))[0:P, 0:T * 2 * (E + 1)].rearrange("p (t i e) -> p t i e", t=T, i=2)
                for i in range(2):
                    for c in chunks(t):
                        ins = mm(o[:, t, i, :], probT[:, k % 2, i, c, :], va[:, t - 1 + c, 2 * u + i, :],
                                 start=(c == chunks(t)[0]), stop=(c == 1))
                if t == T - 1:
                    ins.then_inc(fullsem(("ao", u)), 1)

            def attention(n, u):
                for k in range(u * T, (u + 1) * T + (u == NU - 1)):
                    if k < len(UNITS):
                        scores(n, k)
                    if k > 0:
                        transposes(n, k - 1)
                        values(n, k - 1)

            def ssm(n, u):
                c = u // (NU // 2)
                pe.wait_ge(hX_ready.sem, hX_ready.now(n, NU + u + 1))
                if u == 0:
                    pe.wait_ge(elu_ready.sem, elu_ready.now(n, 4))
                for s, (kt, i0, ni) in enumerate(SC):
                    o = open_tile(n, ("ssm", u, s))[0:P, 0:ni * (L - kt * P)].rearrange("p (i q) -> p i q", i=ni)
                    mm(o, skT[:, c, kt * P:(kt + 1) * P], hX[:, (NU + u) % NX, i0:i0 + ni, kt * P:L],
                       start=True, stop=True).then_inc(fullsem(("ssm", u, s)), 1)
                for s in range(len(SC)):
                    wait_read(pe, n, ("ssm", u, s))
                o = open_tile(n, ("so", u))[0:P, 0:T * 2 * (E + 1)].rearrange("p (t i e) -> p t i e", t=T, i=2)
                for i in range(2):
                    for t in range(T):
                        for kt in range(t + 1):
                            ins = mm(o[:, t, i, :], att[kt][:, i, (t - kt) * P:(t - kt + 1) * P],
                                     vs[:, kt, 2 * u + i, :], start=(kt == 0), stop=(kt == t))
                ins.then_inc(fullsem(("so", u)), 1)

            def tail(n):
                flat = lambda b: b[:, :, :, :].rearrange("p t h e -> p t (h e)")

                def wait_both(name):
                    for c in range(2):
                        wait_read(pe, n, (name, c))

                wait_read(pe, n, ("so", NU - 1))
                for c in range(2):
                    transpose_tiles(n, "soT", flat(so), c)
                wait_both("soT")
                for pair in range(2):
                    linear(n, "so2", tB, wsout, pair)
                for c in range(2):
                    transpose_tiles(n, "aoT", flat(ao), c)
                wait_both("aoT")
                for pair in range(2):
                    linear(n, "sum", tA, wproj, pair)
                wait_both("sum")
                for c in range(2):
                    transpose_tiles(n, "smT", so2, c)
                wait_both("smT")
                for pair in range(2):
                    linear(n, "out", tB, wout, pair)
                pe.wait_ge(x2n_ready.sem, x2n_ready.now(n, 1))
                for c in range(2):
                    transpose_tiles(n, "x2T", xn, c)

            def hidden(n, name, w, xT):
                o = open_tile(n, name)
                for c in range(2):
                    ins = mm(o[:, 0:L], w[0:DC + c, c, :], xT[0:DC + c, c, :], start=(c == 0), stop=(c == 1))
                ins.then_inc(fullsem(name), 1)

            def second(n, name, hid, j, src, w, first):
                wait_read(pe, n, hid)
                for pair, (t0, t1) in enumerate(PAIRS):
                    if first:
                        open_tile(n, name + (pair,))
                    o = at(name + (pair,))
                    for t in range(t0, t1):
                        ins = mm(o[0:P, (t - t0) * D:(t - t0 + 1) * D], src[:, t * P:(t + 1) * P], w,
                                 start=(first and t == t0), stop=(j == NJ - 1), skip_group_check=True)
                    if j == NJ - 1:
                        ins.then_inc(fullsem(name + (pair,)), 1)

            def mlp(n):
                for c in range(2):
                    wait_read(pe, n, ("x2T", c))
                for pair, (t0, t1) in enumerate(PAIRS):
                    o = open_tile(n, ("my", pair))
                    for t in range(t0, t1):
                        mm(o[0:P, (t - t0) * D:(t - t0 + 1) * D], causal[0:1, 0:P], bm2[:, :], start=(t == t0), stop=False,
                           skip_group_check=True)
                for j in range(NJ + 2):
                    if j < NJ:
                        hidden(n, ("mh", j), wm1[:, :, j * 128:(j + 1) * 128], tA)
                    if j >= 2:
                        second(n, ("my",), ("mh", j - 2), j - 2, hmT[:, (j - 2) % NH_, :], wm2[:, j - 2, :], False)
                pe.wait_ge(z_ready.sem, z_ready.now(n, 1))
                for c in range(2):
                    transpose_tiles(n, "zT", xn, c)
                for c in range(2):
                    wait_read(pe, n, ("zT", c))
                o = open_tile(n, ("gate",))
                for t in range(T):
                    for c in range(2):
                        ins = mm(o[0:P, t * NE:(t + 1) * NE], zT[0:DC + c, c, t * P:(t + 1) * P], wg[0:DC + c, c, :],
                                 start=(c == 0), stop=(c == 1))
                ins.then_inc(fullsem(("gate",)), 1)
                pe.wait_ge(comb_ready.sem, comb_ready.now(n, 1))
                o = open_tile(n, ("combT",))
                for t in range(T):
                    ins = nc.tensor.transpose(o[0:NE, t * P:(t + 1) * P], comb[:, t, :], ident[0:P, 0:P])
                ins.then_inc(fullsem(("combT",)), 1)

            def experts(n, e):
                if e == 0:
                    wait_read(pe, n, ("combT",))
                    for pair, (t0, t1) in enumerate(PAIRS):
                        o = open_tile(n, ("cb", pair))
                        for t in range(t0, t1):
                            ins = mm(o[0:P, (t - t0) * D:(t - t0 + 1) * D], combT[:, t * P:(t + 1) * P], b2s[:, :],
                                     start=True, stop=True)
                        ins.then_inc(fullsem(("cb", pair)), 1)
                for k in range(e * NJ, (e + 1) * NJ if e < NE else NE * NJ + 2):
                    if e < NE:
                        hidden(n, ("hid", e, k % NJ), w1[:, :, e, (k % NJ) * 128:(k % NJ + 1) * 128], zT)
                    if k >= 2:
                        e_, j = divmod(k - 2, NJ)
                        second(n, ("ye", e_), ("hid", e_, j), j, hT[:, (k - 2) % NH_, :], w2[:, e_, j, :], j == 0)

            pe.wait_ge(weights_a, 16 * NWA)
            pe.wait_ge(setup, NSETUP)
            run_schedule(dict(front=front, qk=qk, attention=attention, ssm=ssm, tail=tail, mlp=mlp, experts=experts), pe,
                         lambda: pe.wait_ge(weights_b, 16 * NWB))

        @block.scalar
        def _(act):
            A = nc.scalar.activation

            def copyT(n, name, dst):
                for c in range(2):
                    wait_full(act, n, (name, c))
                    A(dst[0:DC, c, :], at((name, c))[0:DC, 0:L], ACT.Copy).then_inc(readsem((name, c)), 1)

            def front(n):
                act.wait_ge(h0_done.sem, h0_done.before(n, 1))
                for t, m in ((0, P), (1, I1)):
                    wait_full(act, n, ("tok", t))
                    A(h0[0:m, t, :], at(("tok", t))[0:m, 0:D], ACT.Copy).then_inc(readsem(("tok", t)), 1)
                copyT(n, "xnT", tA)

            def qk(n):
                for m, dst in enumerate((qT, qT, kT, kT)):
                    wait_full(act, n, ("qk", m))
                    A(dst[:, m % 2, :], at(("qk", m))[0:DC, 0:L], ACT.Copy,
                      scale=E ** -0.5 if dst is qT else 1.0).then_inc(readsem(("qk", m)), 1)
                for m in range(4):
                    name = ("qk", 4 + m)
                    wait_full(act, n, name)
                    act.wait_ge(elu_ready.sem, elu_ready.now(n, m) if m else elu_ready.before(n, 4))
                    A(elue[:, :], at(name)[0:DC, 0:L], ACT.Exp).then_inc(elu_exp.sem, 1)
                for t in range(T):
                    name = ("v", t)
                    wait_full(act, n, name)
                    o = at(name)[0:P, 0:2 * D].rearrange("p (a h e) -> p a h e", a=2, h=H)
                    A(va[:, t, :, 0:E], o[:, 0, :, :], ACT.Copy)
                    A(vs[:, t, :, 0:E], o[:, 1, :, :], ACT.Copy).then_inc(readsem(name), 1)

            def attention(n, u):
                for k in range(u * T, (u + 1) * T):
                    _, t = UNITS[k]
                    w = P if t == 0 else W
                    act.wait_ge(nmax_ready.sem, nmax_ready.now(n, k + 1))
                    if k >= 2:
                        wait_full(act, n, ("probT", k - 2))
                    o = at(("score", k))[0:P, 0:2 * w].rearrange("p (i k) -> p i k", i=2)
                    for i in range(2):
                        ins = A(prob[:, k % 2, i, 2 * P - w:2 * P], o[:, i, :], ACT.Exp, bias=nmax[:, k % 2, i:i + 1])
                    ins.then_inc(readsem(("score", k)), 1)

            def ssm(n, u):
                pass

            def tail(n):
                copyT(n, "soT", tB)
                for pair, (t0, t1) in enumerate(PAIRS):
                    wait_full(act, n, ("so2", pair))
                    A(so2[:, t0:t1, :], at(("so2", pair))[0:P, 0:(t1 - t0) * D].rearrange("p (t d) -> p t d", d=D), ACT.Copy)\
                        .then_inc(readsem(("so2", pair)), 1)
                copyT(n, "aoT", tA)
                copyT(n, "smT", tB)
                copyT(n, "x2T", tA)

            def mlp(n):
                for j in range(NJ):
                    wait_full(act, n, ("mh", j))
                    A(hmT[:, j % NH_, :], at(("mh", j))[:, 0:L], ACT.Gelu).then_inc(readsem(("mh", j)), 1)
                copyT(n, "zT", zT)
                wait_full(act, n, ("combT",))
                A(combT[:, :], at(("combT",))[0:NE, 0:L], ACT.Copy).then_inc(readsem(("combT",)), 1)

            def experts(n, e):
                for j in range(NJ if e < NE else 0):
                    name = ("hid", e, j)
                    wait_full(act, n, name)
                    A(hT[:, (e * NJ + j) % NH_, :], at(name)[:, 0:L], ACT.Gelu).then_inc(readsem(name), 1)

            act.wait_ge(setup, NSETUP)
            run_schedule(dict(front=front, qk=qk, attention=attention, ssm=ssm, tail=tail, mlp=mlp, experts=experts), act)

        @block.vector
        def _(dve):
            V = nc.vector
            links = [0]

            def link(n, ins):
                links[0] += 1
                ins.then_inc(linked.sem, 1)
                dve.wait_ge(linked.sem, linked.now(n, links[0]))

            def norm(n, k, src, dst, affine):
                for t in range(T):
                    ins = V.bn_stats(stats[:, t, :], src[:, t, :])
                link(n, ins)
                hold(dve)
                for t in range(T):
                    ins = V.bn_aggr(mv[:, t, :], stats[:, t, :])
                ins.then_inc(var_ready.sem, 1)
                dve.wait_ge(rstd_ready.sem, rstd_ready.now(n, k + 1))
                for t in range(T):
                    ins = V.tensor_scalar(dst[:, t, :], src[:, t, :], mv[:, t, 0:1], rstd[:, t:t + 1], ALU.subtract, ALU.mult)
                if affine is None:
                    return ins
                link(n, ins)
                link(n, V.tensor_tensor(dst[:, :, :], dst[:, :, :], lnw[:, affine, 0:1, :].to_broadcast((P, T, D)), ALU.mult))
                return V.tensor_tensor(dst[:, :, :], dst[:, :, :], lnw[:, affine, 1:2, :].to_broadcast((P, T, D)), ALU.add)

            def add_pairs(n, name, dst, other):
                for pair, (t0, t1) in enumerate(PAIRS):
                    wait_full(dve, n, (name, pair))
                    V.tensor_tensor(dst[:, t0:t1, :], at((name, pair))[0:P, 0:(t1 - t0) * D].rearrange("p (t d) -> p t d", d=D),
                                    other[:, t0:t1, :], ALU.add).then_inc(readsem((name, pair)), 1)

            def wait_pairs(n, name):
                for pair in range(2):
                    wait_read(dve, n, (name, pair))

            def front(n):
                links[0] = 0
                for g in range(3):
                    dve.wait_ge(x_loaded[g].sem, x_loaded[g].now(n, 16))
                    V.tensor_reduce(pooled[:, g, :], xin[:, g % 2, :].rearrange("p (r j w) -> p j r w", j=NP, w=KP),
                                    axis=AX.XY, op=ALU.add).then_inc(x_read.sem, 1)
                dve.wait_ge(x_read.sem, x_read.now(n, 3))
                for g in range(3):
                    V.tensor_tensor(patch[:, g, :, :], pooled[:, g, None, :].to_broadcast((PX, NP, NP)),
                                    patchm[:, :, None].to_broadcast((PX, NP, NP)), ALU.mult).then_inc(patch_ready.sem, 1)
                for t in range(2):
                    wait_read(dve, n, ("tok", t))
                dve.wait_ge(txt_loaded.sem, txt_loaded.now(n, 32))
                link(n, norm(n, 0, h0, y, None))
                norm(n, 1, y, xn, 0).then_inc(xn_ready.sem, 1)

            def qk(n):
                for m in range(4):
                    name = ("qk", 4 + m)
                    dve.wait_ge(elu_exp.sem, elu_exp.now(n, m + 1))
                    V.tensor_scalar(elur[:, :], at(name)[0:DC, 0:L], 0.0, 1e-4, ALU.max, ALU.add).then_inc(readsem(name), 1)
                    wait_read(dve, n, name)
                    if m == 0:
                        dve.wait_ge(hX_ready.sem, hX_ready.before(n, 2 * NU))
                    V.scalar_tensor_tensor((sqT, skT)[m // 2][:, m % 2, :], elue[:, :], 1.0, elur[:, :],
                                           ALU.min, ALU.add).then_inc(elu_ready.sem, 1)
                    dve.wait_ge(elu_ready.sem, elu_ready.now(n, m + 1))

            def attention(n, u):
                for k in range(u * T, (u + 1) * T + (u == NU - 1)):
                    if k < len(UNITS):
                        _, t = UNITS[k]
                        w = P if t == 0 else W
                        wait_full(dve, n, ("score", k))
                        if k >= 2:
                            wait_read(dve, n, ("score", k - 2))
                        V.tensor_reduce(nmax[:, k % 2, :], at(("score", k))[0:P, 0:2 * w].rearrange("p (i k) -> p i k", i=2),
                                        axis=AX.X, op=ALU.max, negate=True).then_inc(nmax_ready.sem, 1)
                    if k > 0:
                        v, t = UNITS[k - 1]
                        wait_full(dve, n, ("probT", k - 1))
                        c0 = 1 if t == 0 else 0
                        o = at(("probT", k - 1))[0:P, 0:4 * P].rearrange("p (i c q) -> p i c q", i=2, c=2)
                        V.tensor_copy(probT[:, (k - 1) % 2, :, c0:2, :], o[:, :, c0:2, :]).then_inc(readsem(("probT", k - 1)), 1)
                        if t == T - 1:
                            normalise(n, ("ao", v), 0.0, ao)

            def normalise(n, name, eps, dst):
                u = name[1]
                wait_full(dve, n, name)
                o = at(name)[0:P, 0:T * 2 * (E + 1)].rearrange("p (t i e) -> p t i e", t=T, i=2)
                link(n, V.tensor_scalar(den[:, :, :], o[:, :, :, E], eps, None, ALU.add))
                link(n, V.reciprocal(den[:, :, :], den[:, :, :]))
                V.tensor_tensor(dst[:, :, 2 * u:2 * u + 2, :], o[:, :, :, 0:E], den[:, :, :, None].to_broadcast((P, T, 2, E)),
                                ALU.mult).then_inc(readsem(name), 1)

            def ssm(n, u):
                for s, (kt, i0, ni) in enumerate(SC):
                    name = ("ssm", u, s)
                    q = L - kt * P
                    wait_full(dve, n, name)
                    V.tensor_tensor(att[kt][:, i0:i0 + ni, :], at(name)[0:P, 0:ni * q].rearrange("p (i q) -> p i q", i=ni),
                                    causal[:, None, 0:q].to_broadcast((P, ni, q)), ALU.mult).then_inc(readsem(name), 1)
                normalise(n, ("so", u), 1e-4 * E ** 0.5, so)

            def tail(n):
                wait_pairs(n, "so2")
                link(n, norm(n, 2, so2, so2, 1))
                add_pairs(n, "sum", so2, so2)
                add_pairs(n, "out", y, y)
                wait_pairs(n, "out")
                norm(n, 3, y, xn, 2).then_inc(x2n_ready.sem, 1)

            def mlp(n):
                V.tensor_tensor(y[:, :, :], y[:, :, :], h0[:, :, :], ALU.add).then_inc(h0_done.sem, 1)
                dve.wait_ge(h0_done.sem, h0_done.now(n, 1))
                dve.wait_ge(stored.sem, stored.before(n, 16))
                add_pairs(n, "my", hres, y)
                wait_pairs(n, "my")
                norm(n, 4, hres, xn, None).then_inc(z_ready.sem, 1)
                wait_full(dve, n, ("gate",))
                V.tensor_copy(gate[:, :, :], at(("gate",))[0:P, 0:T * NE].rearrange("p (t e) -> p t e", t=T)).then_inc(readsem(("gate",)), 1)
                wait_read(dve, n, ("gate",))
                hold(dve)
                for t in range(T):
                    ins = V.max(top8[:, t, :], gate[:, t, :])
                link(n, ins)
                hold(dve)
                for t in range(T):
                    ins = V.max_index(idx8[:, t, :], top8[:, t, :], gate[:, t, :])
                link(n, ins)
                link(n, V.tensor_copy(idxf[:, :, :], idx8[:, :, :]))
                for t in range(T):
                    V.tensor_scalar(comb[:, t, :], iota8[:, :], idxf[:, t, 0:1], top8[:, t, 0:1], ALU.is_equal, ALU.mult)
                    ins = V.tensor_scalar(comb2[:, t, :], iota8[:, :], idxf[:, t, 1:2], top8[:, t, 1:2], ALU.is_equal, ALU.mult)
                link(n, ins)
                V.tensor_tensor(comb[:, :, :], comb[:, :, :], comb2[:, :, :], ALU.add).then_inc(comb_ready.sem, 1)
                assert links[0] == VLINKS, links[0]

            def experts(n, e):
                if e == 0:
                    dve.wait_ge(comb_ready.sem, comb_ready.now(n, 1))
                    for pair, (t0, t1) in enumerate(PAIRS):
                        wait_full(dve, n, ("cb", pair))
                        V.tensor_tensor(hres[:, t0:t1, :], at(("cb", pair))[0:P, 0:(t1 - t0) * D].rearrange("p (t d) -> p t d", d=D),
                                        hres[:, t0:t1, :], ALU.add).then_inc(readsem(("cb", pair)), 1)
                    return
                for pair, (t0, t1) in enumerate(PAIRS):
                    name = ("ye", e - 1, pair)
                    wait_full(dve, n, name)
                    wait_read(dve, n, ("ye", e - 2, pair) if e > 1 else ("cb", pair))
                    for t in range(t0, t1):
                        ins = V.scalar_tensor_tensor(hres[:, t, :], at(name)[0:P, (t - t0) * D:(t - t0 + 1) * D], comb[:, t, e - 1:e],
                                                     hres[:, t, :], ALU.mult, ALU.add)
                    ins.then_inc(readsem(name), 1)

            dve.wait_ge(weights_a, 16 * NWA)
            dve.wait_ge(setup, NSETUP)
            run_schedule(dict(front=front, qk=qk, attention=attention, ssm=ssm, tail=tail, mlp=mlp, experts=experts), dve)


_INS = ['x', 'txt', 'L0_tok_channel_weights', 'L0_attn_ln1_g', 'L0_attn_ln1_b', 'L0_attn_attn_qkv_w', 'L0_attn_attn_qkv_b',
        'L0_attn_attn_proj_w', 'L0_attn_attn_proj_b', 'L0_attn_ssm_qkv_w', 'L0_attn_ssm_qkv_b', 'L0_attn_ssm_out_w',
        'L0_attn_ssm_out_b', 'L0_attn_ssm_ln_g', 'L0_attn_ssm_ln_b', 'L0_attn_out_w', 'L0_attn_out_b', 'L0_attn_mlp_w1',
        'L0_attn_mlp_b1', 'L0_attn_mlp_w2', 'L0_attn_mlp_b2', 'L0_attn_lnm_g', 'L0_attn_lnm_b',
        'L0_ffn_Wg', 'L0_ffn_bg', 'L0_ffn_W1', 'L0_ffn_b1', 'L0_ffn_W2', 'L0_ffn_b2']
_OUTS = [((16, 324, 192), 'float32')]


def kernel(**inputs):
    import numpy as _np
    import concourse.bacc as _bacc
    from concourse import mybir as _mybir
    from concourse.bass_utils import run_bass_kernel_spmd as _run

    nc = _bacc.Bacc("TRN2", target_bir_lowering=False, num_devices=1)
    arrays, args = {}, []
    for name in _INS:
        a = _np.ascontiguousarray(inputs[name])
        arrays[f"in_{name}_dram"] = a
        args.append(nc.dram_tensor(f"in_{name}_dram", a.shape, _mybir.dt.from_np(a.dtype), kind="ExternalInput").ap())
    for i, (shape, dtype) in enumerate(_OUTS):
        dt = _mybir.dt.from_np(_np.dtype(dtype))
        args.append(nc.dram_tensor(f"out_{i}_dram", shape, dt, kind="ExternalOutput").ap())
    early_fusion_moe_kernel(nc, *args)
    r = _run(nc, [arrays], core_ids=[0])
    return r.results[0]["out_0_dram"]
```

```python
import concourse.bass as bass
from concourse import mybir
from contextlib import ExitStack


def early_fusion_moe_kernel(nc, x, txt, cw, ln1_g, ln1_b, qkv_w, qkv_b, proj_w, proj_b,
                            sqkv_w, sqkv_b, sout_w, sout_b, sln_g, sln_b, out_w, out_b,
                            mlp_w1, mlp_b1, mlp_w2, mlp_b2, lnm_g, lnm_b,
                            Wg, bg, W1, b1, W2, b2, out):
    fp32 = mybir.dt.float32
    fp16 = mybir.dt.float16
    bf16 = mybir.dt.bfloat16
    u32 = mybir.dt.uint32
    ALU = mybir.AluOpType
    ACT = mybir.ActivationFunctionType
    AX = mybir.AxisListType

    S, C, IMG, _ = x.shape
    D = cw.shape[1]
    KP = 16
    NP = IMG // KP
    IT = NP * NP
    TX = txt.shape[1]
    L = IT + TX
    T = 3
    P = L // T
    I1 = IT - P
    H = 12
    E = D // H
    HC = H // 2
    NU = H // 2
    WIN = 64
    W = P + WIN - 1
    DC = D // 2
    DA = 128
    DB = D - DA
    HID = mlp_w1.shape[1]
    NJ = HID // 128
    NE = Wg.shape[1]
    GC = C // 3
    PX = GC * NP * 2
    RW = IMG * KP // 2
    EPS = 1e-5
    FAR = -1e9


    ctx = ExitStack()
    with ctx:
        def sb(name, shape, dt=fp32):
            return ctx.enter_context(nc.sbuf_tensor(name, shape, dt))

        def sem(name):
            return ctx.enter_context(nc.semaphore(name))

        cwrep = sb("cwrep", [PX, 3, D])
        wqk = sb("wqk", [128, 4, 4 * D], fp16)
        wv = sb("wv", [128, 4, 2 * D], fp16)
        wproj = sb("wproj", [128, 4, D], fp16)
        wsout = sb("wsout", [128, 4, D], fp16)
        wout = sb("wout", [128, 4, D], fp16)
        wm1 = sb("wm1", [128, 4, HID], fp16)
        wm2 = sb("wm2", [128, 2, NJ * D], fp16)
        wg = sb("wg", [128, 4, NE], fp16)
        w1 = sb("w1", [128, 4, NE, HID], fp16)
        w2 = sb("w2", [128, 2, NE, NJ * D], fp16)
        bv, bproj, bsout, bout, bm2 = 0, 2 * D, 3 * D, 4 * D, 5 * D
        bgate = 6 * D
        bexp = 6 * D + NE
        NBR = bexp + NE * D
        brow = sb("brow", [33, NBR], fp16)
        ones = sb("ones", [33, P], fp16)
        bqk = sb("bqk", [DC, 8])
        bq4 = sb("bq4", [DC, 2])
        bneg = sb("bneg", [DC, 4])
        bpos = sb("bpos", [DC, 4])
        bh = sb("bh", [128, NE + 1, NJ])
        lnw = sb("lnw", [P, 3, 2, D])
        ident = sb("ident", [128, 128])
        ident16 = sb("ident16", [128, 128], fp16)
        identb = sb("identb", [128, 128], bf16)
        band = sb("band", [P, W], bf16)
        causal = sb("causal", [P, P])
        headm = sb("headm", [DC, HC])
        patchm = sb("patchm", [PX, NP])
        iota8 = sb("iota8", [P, NE])
        mhalf = sb("mhalf", [P, T])

        xin = sb("xin", [PX, 2, RW // 2])
        pooled = sb("pooled", [PX, 6, NP])
        shared = sb("shared", [PX, 8 * P])
        patch = shared[:, 0:3 * IT].rearrange("p (g i j) -> p g i j", g=3, i=NP)
        elur = shared[0:DC, 0:2 * L].rearrange("p (m l) -> p m l", m=2)
        probT = shared[0:P, :].rearrange("p (m i c q) -> p m i c q", m=2, i=2, c=2)
        h0 = sb("h0", [P, T, D])
        y = sb("y", [P, T, D])
        hx = sb("hx", [P, T, D])
        xn = sb("xn", [P, T, D])
        stats = sb("stats", [P, T, 6])
        mv = sb("mv", [P, T, 2])
        rstd = sb("rstd", [P, T])
        stats4, mv4, rstd4 = sb("stats4", [P, T, 6]), sb("mv4", [P, T, 2]), sb("rstd4", [P, T])
        x16 = sb("x16", [P, T, 2 * D], fp16)
        xT = sb("xT", [128, 2, 3, L], fp16)
        zT = sb("zT", [128, 3, L], fp16)
        qT = sb("qT", [DC, 2, L])
        kT = sb("kT", [DC, 2, L])
        sqT = sb("sqT", [DC, 2, L])
        skT = sb("skT", [DC, 2, L])
        NX = 3
        hX = sb("hX", [DC, NX, 2, L])
        va = sb("va", [P, T, H, E + 1])
        vs = sb("vs", [P, T, H, E + 1])
        nmax = sb("nmax", [P, 2, T, 2])
        prob = sb("prob", [P, 2, T, 2, 2 * P])
        state = sb("state", [DC, 2, 2, HC, E + 1])
        NS = 2
        att = shared[0:P, :].rearrange("p (k m i q) -> p k m i q", k=NS, m=2, i=2)
        den = sb("den", [P, T, HC])
        both = sb("both", [P, 2 * T * D])
        ao, so = (both[:, m * T * D:(m + 1) * T * D].rearrange("p (t h e) -> p t h e", t=T, h=H) for m in range(2))
        sktok = both[:, T * D:T * D + 2 * D].rearrange("p (t d) -> p t d", t=2)
        elue = both[0:DC, 0:2 * L].rearrange("p (m l) -> p m l", m=2)
        brow32 = both[0:33, 0:6 * D]
        bg32 = sb("bg32", [33, NE])
        bexp32 = hX[0:33].rearrange("p x i l -> p (x i l)")[:, 0:NE * D]
        so2 = xn
        NR = 4
        hm = sb("hm", [128, NR, L])
        hm16 = sb("hm16", [128, NR, 2, L], fp16)
        NM = 2
        bm = sb("bm", [128, NM, L])
        bm16 = sb("bm16", [128, NM, 2, L], fp16)
        stage = [hm[:, :, :].rearrange("p r l -> p (r l)"),
                 hm16[:, :, :, :].rearrange("p r m l -> p (r m l)").bitcast(fp32)]
        hres = sb("hres", [P, T, D])
        gate = sb("gate", [P, T, NE])
        top8 = sb("top8", [P, T, 8])
        idx8 = sb("idx8", [P, T, 8], u32)
        idxf = sb("idxf", [P, T, 8])
        comb = sb("comb", [P, T, NE])
        comb2 = sb("comb2", [P, T, NE])

        bank = [ctx.enter_context(nc.psum_tensor(f"bank{i}", [128, 512], fp32)) for i in range(8)]

        ring_a, acc_a, ring_h, ring_y = (0, 1, 2), 7, (3, 4), (5, 6)
        PAIRS = ((0, 2), (2, 3))
        UNITS = [(u, t) for u in range(NU) for t in range(T)]
        NSJ = len(UNITS) // 2
        UC = NU // 2
        LATE = NSJ
        LAG, LAGM = NR - 1, NM - 1
        place, turn = {}, [0] * 8

        def plan(name, b):
            place[name] = (b, turn[b])
            turn[b] += 1

        ring = [0]

        def plan_a(*names):
            for name in names:
                plan(name, ring_a[ring[0] % 3])
                ring[0] += 1

        plan_a(("tok", 0), ("tok", 1), ("xT", 0))
        plan_a(*[("qk", m) for m in range(4)])
        plan_a(*[("v", t) for t in range(T)])
        plan_a(*[("qk", m) for m in range(4, 8)])
        for c in range(2):
            plan(("ao", c), acc_a)
        for u in range(NU + 1):
            if u < NU:
                plan_a(*[("score", u * T + t) for t in range(T)])
            if u > 0:
                plan_a(*[("probT", (u - 1) * T + t) for t in range(T)])
        plan_a(("skt",), ("state",))
        plan_a(*[("ssm", k) for k in range(NSJ)])
        for c in range(2):
            plan(("so", c), acc_a)
        plan_a(("xT", 1), ("so2", 0), ("so2", 1), ("xT", 2), ("sum", 0), ("sum", 1), ("xT", 3), ("out", 0), ("out", 1), ("xT", 4))
        for j in range(NJ):
            plan(("hid", NE, j), ring_a[j % 2])
        plan(("ye", NE, 0), acc_a)
        plan(("ye", NE, 1), ring_a[2])
        for name in (("xT", 5), ("gate",)):
            plan(name, acc_a)
        for e in range(NE):
            for j in range(NJ):
                plan(("hid", e, j), ring_h[j % 2])
            for pair in range(2):
                plan(("ye", e, pair), ring_y[pair])

        class Count:
            def __init__(self, name, per):
                self.sem, self.per = sem(name), per
                counts.append(self)

            def now(self, n, k):
                return n * self.per + (self.per + k)

            def before(self, n, k):
                return n * self.per + k

        counts = []
        full = [Count(f"bank{b}_full", turn[b]) for b in range(8)]
        read = [Count(f"bank{b}_read", turn[b]) for b in range(8)]

        def wait_full(eng, n, name):
            b, k = place[name]
            eng.wait_ge(full[b].sem, full[b].now(n, k + 1))

        def wait_read(eng, n, name):
            b, k = place[name]
            eng.wait_ge(read[b].sem, read[b].now(n, k + 1))

        def wait_free(eng, n, name):
            b, k = place[name]
            eng.wait_ge(read[b].sem, read[b].now(n, k) if k else read[b].before(n, turn[b]))

        def at(name):
            return bank[place[name][0]]

        def fullsem(name):
            return full[place[name][0]].sem

        def readsem(name):
            return read[place[name][0]].sem

        NQ = NE * NJ + LAG - 1

        def seconds(q):
            return [k for k in (q - LAG, q - LAG + 1) if 0 <= k < NE * NJ and (k % NJ == NJ - 1) == (k == q - LAG + 1)]

        NSETUP = 27
        FIRST_LINKS, BLOCK_LINKS, GATE_LINKS = 12, 15, 7
        STEPS = [("ssm_state", None, 1, 1)]
        for k in range(NSJ + 1):
            STEPS += [("ssm", k, 1, 1)]
            if k < 6:
                STEPS += [("reduce", k, 0, 0)]
        STEPS += [("so_T", None, 1, 1), ("so_out", None, 1, 1), ("ao_T", None, 1, 1), ("patches", None, 0, 0), ("proj", None, 1, 2),
                  ("sum_T", None, 1, 1), ("out", None, 1, 1), ("norm3", None, 1, 1), ("norm3b", None, 1, 2), ("x2_T", None, 1, 1)]
        STEPS += [("mlp", j, 1, 1 if j < NJ - 1 else 0) for j in range(NJ + LAGM)]
        STEPS += [("norm4", None, 1, 0), ("tokens", None, 0, 1), ("z", None, 1, 2), ("norm0", None, 0, 0), ("z_T", None, 1, 2),
                  ("norm1", None, 0, 1), ("gate", None, 1, 2), ("norm1b", None, 0, 3), ("x_T", None, 0, 1),
                  ("qk", 0, 0, 2), ("values", None, 0, 0), ("qk", 1, 0, 0)]
        for u in range(NU + 1):
            if u < NU:
                STEPS += [("scores", u, 0, 1 if u else 0)]
            if u > 0:
                STEPS += [("attend0", u - 1, 0, 1), ("attend1", u - 1, 0, 0), ("attend2", u - 1, 0, 0)]
        at_gate = [name for name, *_ in STEPS].index("gate")
        QA = sum(moe for *_, moe in STEPS[at_gate:])

        def run_schedule(stage, eng, between=None):
            def turn(i):
                def now(behind):
                    return not isinstance(i, int) or 0 <= i - behind < S

                behind, q = 2, QA
                for at_step, (name, k, b, moe) in enumerate(STEPS):
                    if now(b):
                        if k is None:
                            stage[name](i - b if b else i)
                        else:
                            stage[name](i - b if b else i, k)
                        if isinstance(i, int) and i == 0 and between:
                            between(name, k)
                    if name == "gate":
                        assert q >= NQ, "the experts of sample i - 2 are through"
                        behind, q = 1, 0
                    for _ in range(moe):
                        if now(behind) and q < NQ:
                            stage["moe"](i - behind, q)
                        q += 1

            turn(0)
            turn(1)
            with eng.Fori(2, S) as i:
                turn(i)
            turn(S)
            turn(S + 1)

        setup = sem("setup")
        weights = sem("weights")
        split_hi = sem("split_hi")
        split_lo = sem("split_lo")
        piece = [sem(f"piece{i}") for i in range(2)]
        bias_split = sem("bias_split")
        bias_hi = sem("bias_hi")
        x_loaded = [Count(f"x_loaded{h}", 48) for h in range(2)]
        x_read = Count("x_read", 6)
        txt_loaded = Count("txt_loaded", 32)
        h0_done = Count("h0_done", 1)
        patch_ready = Count("patch_ready", 3)
        var_ready = Count("var_ready", 5)
        eps_added = Count("eps_added", 5)
        rstd_ready = Count("rstd_ready", 5)
        x16_ready = Count("x16_ready", 6)
        elu_exp = Count("elu_exp", 4)
        elu_ready = Count("elu_ready", 4)
        hX_ready = Count("hX_ready", 2 * NU)
        nmax_ready = Count("nmax_ready", len(UNITS))
        lo_ready = Count("lo_ready", NE * NJ)
        blo_ready = Count("blo_ready", NJ)
        comb_ready = Count("comb_ready", 1)
        stored = Count("stored", 16)
        first, second_part, gating = Count("first", FIRST_LINKS), Count("second_part", BLOCK_LINKS), Count("gating", GATE_LINKS)
        held = sem("held")

        def moments_of(k):
            return (stats4, mv4, rstd4) if k == 4 else (stats, mv, rstd)

        def slot_xT(k):
            return (1, 0, 1, 0, 0)[k]

        def hold(eng):
            eng.sem_inc(held, 1)

        def pieces():
            def width(dst, src, n):
                yield "wide", n, (dst[:, 0], dst[:, 1]), [(slice(0, 128), src[0:DA])]
                yield "rest", n, (dst[:, 2], dst[0:DB, 3]), [(slice(0, DB), src[DA:D]), (slice(DB, 128), src[DA:D])]

            for m in range(2):
                yield from width(wqk[:, :, m * D:(m + 1) * D], qkv_w[:, m * D:(m + 1) * D], D)
            for m in range(2):
                yield from width(wqk[:, :, (2 + m) * D:(3 + m) * D], sqkv_w[:, m * D:(m + 1) * D], D)
            yield from width(wv[:, :, 0:D], qkv_w[:, 2 * D:3 * D], D)
            yield from width(wv[:, :, D:2 * D], sqkv_w[:, 2 * D:3 * D], D)
            for dst, src in ((wsout, sout_w), (wproj, proj_w), (wout, out_w)):
                yield from width(dst, src, D)
            yield from width(wm1, mlp_w1, HID)
            yield from width(wg, Wg, NE)
            for half in range(2):
                j = slice(half * NJ // 2 * D, (half + 1) * NJ // 2 * D)
                yield "rows", NJ // 2 * D, (wm2[:, 0, j], wm2[:, 1, j]), [(slice(0, 128), rows(mlp_w2, half))]

        def expert_pieces(e):
            yield "wide", HID, (w1[:, 0, e], w1[:, 1, e]), [(slice(0, 128), W1[e, 0:DA])]
            yield "rest", HID, (w1[:, 2, e], w1[0:DB, 3, e]), [(slice(0, DB), W1[e, DA:D]), (slice(DB, 128), W1[e, DA:D])]
            for half in range(2):
                j = slice(half * NJ // 2 * D, (half + 1) * NJ // 2 * D)
                yield "rows", NJ // 2 * D, (w2[:, 0, e, j], w2[:, 1, e, j]), [(slice(0, 128), rows(W2[e], half))]

        def rows(w, half):
            n = HID // 2
            return w[half * n:(half + 1) * n, :].rearrange("(j p) d -> p j d", p=128)

        block_pieces = list(pieces())
        NPB = len(block_pieces)
        all_pieces = block_pieces + [p for e in range(NE) for p in expert_pieces(e)]
        landed = [0, 0]
        piece_count = []
        for k, (_, _, _, srcs) in enumerate(all_pieces):
            landed[k % 2] += 16 * len(srcs)
            piece_count.append(landed[k % 2])

        block = ctx.enter_context(nc.Block())

        @block.sync
        def _(sp):
            def load(dst, src):
                sp.dma_start(dst, src).then_inc(weights, 16)
                return 1

            def load_piece(k):
                _, n, _, srcs = all_pieces[k]
                if k >= 2:
                    sp.wait_ge(split_lo, k - 1)
                for part, src in srcs:
                    d = stage[k % 2][part, 0:n]
                    if len(src.shape) == 3:
                        d = d.rearrange("p (j d) -> p j d", d=D)
                    sp.dma_start(d, src).then_inc(piece[k % 2], 16)

            x_v = x.rearrange("s (g c) (i b u r) w -> s u g (c i b) (r w)", g=3, i=NP, b=2, u=2)

            def load_x(n, h, lead):
                sp.wait_ge(x_read.sem, lead[h])
                sp.dma_start(xin[:, h % 2, :], x_v[bass.ds(n, 1), h // 3, h % 3, :, :].rearrange("s p f -> (s p) f"))\
                    .then_inc(x_loaded[h % 2].sem, 16)

            def load_text(n, lead):
                sp.wait_ge(h0_done.sem, lead[6])
                sp.dma_start(h0[I1:P, 1, :], txt[bass.ds(n, 1), 0:P - I1, :].rearrange("s p d -> (s p) d")).then_inc(txt_loaded.sem, 16)
                sp.dma_start(h0[:, 2, :], txt[bass.ds(n, 1), P - I1:TX, :].rearrange("s p d -> (s p) d")).then_inc(txt_loaded.sem, 16)

            def load_sample(n, lead):
                for h in range(6):
                    load_x(n, h, lead)
                load_text(n, lead)

            def store_sample(n, lead):
                for b, v in zip(ring_y, lead):
                    sp.wait_ge(read[b].sem, v)
                sp.dma_start(out[bass.ds(n, 1), :, :].rearrange("s (t p) d -> p (s t) d", t=T), hres[:, :, :]).then_inc(stored.sem, 16)

            def leads(n):
                return [x_read.before(n, 5), x_read.before(n, 6)] + [x_read.now(n, h - 1) for h in range(2, 6)] + [h0_done.before(n, 1)]

            row = lambda b, r=1: b.rearrange("(o d) -> o d", o=1).to_broadcast((r, b.shape[0]))
            for r in (0, 32):
                for o, b in ((bv, qkv_b[2 * D:3 * D]), (bv + D, sqkv_b[2 * D:3 * D]), (bproj, proj_b), (bsout, sout_b),
                             (bout, out_b), (bm2, mlp_b2)):
                    load(brow32[r:r + 1, o:o + b.shape[0]], row(b))
                load(bg32[r:r + 1, :], row(bg))
                load(bexp32[r:r + 1, :], row(b2.rearrange("e d -> (e d)")))
            for k, (g_, b_) in enumerate(((ln1_g, ln1_b), (sln_g, sln_b), (lnm_g, lnm_b))):
                load(lnw[:, k, 0, :], row(g_, P))
                load(lnw[:, k, 1, :], row(b_, P))
            for g in range(3):
                for c in range(GC):
                    load(cwrep[c * 2 * NP:(c + 1) * 2 * NP, g, :], cw[g * GC + c:g * GC + c + 1, :].to_broadcast((2 * NP, D)))
            with nc.allow_non_contiguous_dma(reason="biases to columns, once"):
                for k, b in enumerate((qkv_b, sqkv_b)):
                    load(bqk[:, 4 * k:4 * k + 4], b[0:2 * D].rearrange("(m p) -> p m", p=DC))
                load(bh[:, 0:NE, :], b1.rearrange("e (j p) -> p e j", p=128))
                load(bh[:, NE, :], mlp_b1.rearrange("(j p) -> p j", p=128))
            for k in range(NPB):
                load_piece(k)
                if k < 2:
                    load_x(0, k, leads(0))
            for h in range(2, 6):
                load_x(0, h, leads(0))
            load_text(0, leads(0))
            for k in range(NPB, len(all_pieces)):
                load_piece(k)
            load_sample(1, leads(1))
            with sp.Fori(2, S) as i:
                load_sample(i, [sp.snap(v) for v in leads(i)])
                store_sample(i - 2, [sp.snap(read[b].now(i - 2, turn[b])) for b in ring_y])
            for n in (S - 2, S - 1):
                store_sample(n, [read[b].now(n, turn[b]) for b in ring_y])
            sp.wait_ge(stored.sem, stored.now(S - 1, 16))

        NWEIGHTS = 16 + 6 + 12 + 4

        @block.gpsimd
        def _(pool):
            steps = [0]

            def step(ins):
                steps[0] += 1
                ins.then_inc(setup, 1)
                pool.wait_ge(setup, steps[0])

            for c in counts:
                pool.sem_inc(c.sem, c.per)
            step(pool.memset(patchm[:, :], 0.0))
            for c in range(GC):
                for b in range(2):
                    step(pool.affine_select(out=patchm[:, :], in_=patchm[:, :], compare_op=ALU.not_equal, fill=1.0,
                                            base=-(2 * NP * c + b), pattern=[[-2, NP]], channel_multiplier=1))
            step(pool.memset(ident[:, :], 0.0))
            step(pool.affine_select(out=ident[:, :], in_=ident[:, :], compare_op=ALU.not_equal, fill=1.0,
                                    base=0, pattern=[[-1, 128]], channel_multiplier=1))
            step(pool.tensor_copy(identb[:, :], ident[:, :]))
            step(pool.tensor_copy(ident16[:, :], ident[:, :]))
            step(pool.memset(ones[:, :], 1.0))
            step(pool.memset(mhalf[:, :], -0.5))
            step(pool.memset(band[:, :], 0.0))
            step(pool.affine_select(out=band[:, :], in_=band[:, :], compare_op=ALU.is_ge, fill=FAR,
                                    base=0, pattern=[[1, W]], channel_multiplier=-1))
            step(pool.affine_select(out=band[:, :], in_=band[:, :], compare_op=ALU.is_ge, fill=FAR,
                                    base=WIN - 1, pattern=[[-1, W]], channel_multiplier=1))
            step(pool.memset(causal[:, :], 1.0))
            step(pool.affine_select(out=causal[:, :], in_=causal[:, :], compare_op=ALU.is_ge, fill=0.0,
                                    base=0, pattern=[[1, P]], channel_multiplier=-1))
            step(pool.memset(headm[:, :], 1.0))
            step(pool.affine_select(out=headm[:, :], in_=headm[:, :], compare_op=ALU.is_ge, fill=0.0,
                                    base=0, pattern=[[-E, HC]], channel_multiplier=1))
            step(pool.affine_select(out=headm[:, :], in_=headm[:, :], compare_op=ALU.is_ge, fill=0.0,
                                    base=E - 1, pattern=[[E, HC]], channel_multiplier=-1))
            step(pool.memset(prob[:, :, :, :], 0.0))
            step(pool.memset(va[:, :, :, :], 1.0))
            step(pool.memset(vs[:, :, :, :], 1.0))
            step(pool.iota(iota8[:, :], pattern=[[1, NE]], base=0, channel_multiplier=0, allow_small_or_imprecise_dtypes=True))
            assert steps[0] == NSETUP, steps[0]

            def deviation(n, k):
                pool.wait_ge(var_ready.sem, var_ready.now(n, k + 1))
                hold(pool)
                _, var, r = moments_of(k)
                pool.tensor_scalar(r[:, :], var[:, :, 1], EPS, None, ALU.add).then_inc(eps_added.sem, 1)
                pool.wait_ge(eps_added.sem, eps_added.now(n, k + 1))
                pool.tensor_tensor(r[:, :], r[:, :], mhalf[:, :], ALU.pow).then_inc(rstd_ready.sem, 1)

            def last_reader(k):
                return ("score", T * k + T - 1) if k < NU else ("ssm", (T * (k - NU) + T - 1) // 2)

            def copies(n, k):
                u = k % NU
                src = kT if k < NU else sqT
                if u % UC == 0:
                    if k < NU:
                        wait_read(pool, n, ("qk", 2 + u // UC))
                    else:
                        pool.wait_ge(elu_ready.sem, elu_ready.now(n, 1 + u // UC))
                if k < NX:
                    b, m = place[last_reader(k - NX + 2 * NU)]
                    pool.wait_ge(full[b].sem, full[b].before(n, m + 1))
                else:
                    wait_full(pool, n, last_reader(k - NX))
                hold(pool)
                for i in range(2):
                    h = (2 * u + i) % HC
                    ins = pool.tensor_scalar(hX[:, k % NX, i, :], src[:, u // UC, :], headm[:, h:h + 1], None, ALU.mult)
                ins.then_inc(hX_ready.sem, 1)

            def add_h0(n):
                pool.wait_ge(x16_ready.sem, x16_ready.now(n, 5))
                pool.tensor_tensor(hx[:, :, :], hx[:, :, :], h0[:, :, :], ALU.add).then_inc(h0_done.sem, 1)

            def scores(n, u):
                if 0 < u < NU - NX + 1:
                    copies(n, u + NX - 1)

            def first_copies(n, half):
                if half == 1:
                    for k in range(NX):
                        copies(n, k)

            def ssm_copies(n, k):
                for u in range(NU):
                    if (T * u + T - 1) // 2 == k - 1 and u + NX < NU:
                        copies(n, NU + u + NX)

            def attend(n, u):
                if u >= UC:
                    copies(n, NU + u - UC)

            nothing = lambda n, k=0: None
            run_schedule(dict(ssm_state=nothing, ssm=ssm_copies, reduce=nothing, so_T=nothing, so_out=lambda n: deviation(n, 2),
                              ao_T=nothing, patches=nothing, proj=nothing, sum_T=nothing, out=nothing, norm3=lambda n: deviation(n, 3), norm3b=nothing,
                              x2_T=add_h0, mlp=nothing, tokens=nothing, norm4=lambda n: deviation(n, 4), norm0=lambda n: deviation(n, 0),
                              z=nothing, norm1=lambda n: deviation(n, 1), z_T=nothing, gate=nothing, norm1b=nothing, 
                              x_T=nothing, qk=first_copies, values=nothing, scores=scores, attend0=attend, attend1=nothing,
                              attend2=nothing, moe=nothing), pool)

        @block.tensor
        def _(pe):
            mm = nc.tensor.matmul

            def open_tile(n, name):
                wait_free(pe, n, name)
                return at(name)

            def transpose_split(n, k):
                pe.wait_ge(x16_ready.sem, x16_ready.now(n, k + 1))
                o = open_tile(n, ("xT", k))[:, :].bitcast(fp16)
                for t in range(T):
                    for part in range(3):
                        ins = nc.tensor.transpose(o[:, part * L + t * P:part * L + (t + 1) * P],
                                                  x16[:, t, part * DA:(part + 1) * DA], ident16[0:P, 0:P])
                ins.then_inc(fullsem(("xT", k)), 1)

            def terms(a, b):
                return ((a(0, 128, 0), b(0, 128, 0)), (a(0, 128, 1), b(0, 128, 0)), (a(0, 128, 0), b(0, 128, 1)),
                        (a(0, 128, 2), b(0, 128, 2)), (a(0, DB, 2), b(0, DB, 3)))

            def token_major(o, k_xT, t, w, c, bias, start=True):
                parts = terms(lambda r0, r1, m: k_xT[r0:r1, m, t * P:(t + 1) * P], lambda r0, r1, m: w[r0:r1, m, c])
                mm(o, ones[:, :], brow[:, bias:bias + c.stop - c.start], start=start, stop=False, skip_group_check=True)
                for i, (a, b) in enumerate(parts):
                    ins = mm(o, a, b, start=False, stop=(i == 4), skip_group_check=True)
                return ins

            def feature_major(o, k_xT, w, c):
                parts = terms(lambda r0, r1, m: k_xT[r0:r1, m, :], lambda r0, r1, m: w[r0:r1, m, c])
                for i, (a, b) in enumerate(parts):
                    ins = mm(o, b, a, start=(i == 0), stop=(i == 4))
                return ins

            def linear(n, name, k, w, bias):
                wait_read(pe, n, ("xT", k))
                for pair, (t0, t1) in enumerate(PAIRS):
                    o = open_tile(n, (name, pair))
                    for t in range(t0, t1):
                        ins = token_major(o[0:P, (t - t0) * D:(t - t0 + 1) * D], xT[:, slot_xT(k)], t, w, slice(0, D), bias, t == t0)
                    ins.then_inc(fullsem((name, pair)), 1)

            def tokens(n):
                pe.wait_ge(patch_ready.sem, patch_ready.now(n, 3))
                for t, (a, b) in enumerate(((0, P), (P, IT))):
                    o = open_tile(n, ("tok", t))
                    for g in range(3):
                        ins = mm(o[0:b - a, 0:D], patch[:, g, :, :].rearrange("p i j -> p (i j)")[:, a:b],
                                 cwrep[:, g, :], start=(g == 0), stop=(g == 2))
                    ins.then_inc(fullsem(("tok", t)), 1)

            def qk(n, half):
                if half == 0:
                    wait_read(pe, n, ("xT", 0))
                for m in range(4 * half, 4 * half + 4):
                    o = open_tile(n, ("qk", m))
                    feature_major(o[0:DC, 0:L], xT[:, slot_xT(0)], wqk, slice(m * DC, (m + 1) * DC)).then_inc(fullsem(("qk", m)), 1)

            def values(n):
                for t in range(T):
                    o = open_tile(n, ("v", t))
                    token_major(o[0:P, 0:2 * D], xT[:, slot_xT(0)], t, wv, slice(0, 2 * D), bv).then_inc(fullsem(("v", t)), 1)

            def chunks(t):
                return (1,) if t == 0 else (0, 1)

            def scores(n, u):
                c = u // UC
                pe.wait_ge(hX_ready.sem, hX_ready.now(n, u + 1))
                if u % UC == 0:
                    wait_read(pe, n, ("qk", c))
                for t in range(T):
                    k = u * T + t
                    o = open_tile(n, ("score", k))
                    w = P if t == 0 else W
                    o = o[0:P, 0:2 * w].rearrange("p (i k) -> p i k", i=2)
                    mm(o, identb[0:P, 0:P], band[:, None, W - w:W].to_broadcast((P, 2, w)), start=True, stop=False)
                    mm(o, qT[:, c, t * P:(t + 1) * P], hX[:, u % NX, :, (t + 1) * P - w:(t + 1) * P],
                       start=False, stop=True).then_inc(fullsem(("score", k)), 1)

            def transposes(n, k):
                t = k % T
                wait_read(pe, n, ("score", k))
                o = open_tile(n, ("probT", k))[0:P, 0:4 * P].rearrange("p (i c q) -> p i c q", i=2, c=2)
                for i in range(2):
                    for c in chunks(t):
                        ins = nc.tensor.transpose(o[:, i, c, :], prob[:, k // T % 2, t, i, c * P:(c + 1) * P], ident[0:P, 0:P])
                ins.then_inc(fullsem(("probT", k)), 1)

            def head_sums(name):
                return at(name)[0:P, 0:T * HC * (E + 1)].rearrange("p (t h e) -> p t h e", t=T, h=HC)

            def weigh(n, k):
                u, t = UNITS[k]
                wait_read(pe, n, ("probT", k))
                o = head_sums(("ao", u // UC))
                for i in range(2):
                    for c in chunks(t):
                        ins = mm(o[:, t, (2 * u + i) % HC, :], probT[:, k % 2, i, c, :], va[:, t - 1 + c, 2 * u + i, :],
                                 start=(k % (UC * T) == 0 and i == 0 and c == 1), stop=(c == 1), skip_group_check=True)
                if k % (UC * T) == UC * T - 1:
                    ins.then_inc(fullsem(("ao", u // UC)), 1)

            def attend0(n, u):
                transposes(n, u * T)
                transposes(n, u * T + 1)

            def attend1(n, u):
                if u == 0:
                    for t in range(T):
                        wait_read(pe, n, ("v", t))
                if u % UC == 0:
                    open_tile(n, ("ao", u // UC))
                weigh(n, u * T)
                transposes(n, u * T + 2)
                weigh(n, u * T + 1)

            def attend2(n, u):
                weigh(n, u * T + 2)

            def ssm_state(n):
                pe.wait_ge(elu_ready.sem, elu_ready.now(n, 4))
                o = open_tile(n, ("skt",))[0:P, 0:2 * D].rearrange("p (t d) -> p t d", t=2)
                for t in range(2):
                    for c in range(2):
                        ins = nc.tensor.transpose(o[:, t, c * DC:(c + 1) * DC], skT[:, c, t * P:(t + 1) * P], ident[0:DC, 0:DC])
                ins.then_inc(fullsem(("skt",)), 1)
                wait_read(pe, n, ("skt",))
                o = open_tile(n, ("state",))[0:DC, 0:4 * HC * (E + 1)].rearrange("p (t c f) -> p t c f", t=2, c=2)
                for t in range(2):
                    for c in range(2):
                        for kt in range(t + 1):
                            ins = mm(o[:, t, c, :], sktok[:, kt, c * DC:(c + 1) * DC],
                                     vs[:, kt, c * HC:(c + 1) * HC, :].rearrange("p h e -> p (h e)"), start=(kt == 0), stop=(kt == t))
                ins.then_inc(fullsem(("state",)), 1)

            def ssm(n, k):
                if k == NSJ // 2 + 2:
                    ssm_sums(n, LATE)
                if k < NSJ:
                    o = open_tile(n, ("ssm", k))[0:P, 0:4 * P].rearrange("p (m i q) -> p m i q", m=2, i=2)
                    for m in range(2):
                        u, t = UNITS[2 * k + m]
                        if t == 0:
                            pe.wait_ge(hX_ready.sem, hX_ready.now(n, NU + u + 1))
                        ins = mm(o[:, m], skT[:, u // UC, t * P:(t + 1) * P], hX[:, (NU + u) % NX, :, t * P:(t + 1) * P],
                                 start=True, stop=True)
                    ins.then_inc(fullsem(("ssm", k)), 1)
                for unit in range(2 * (k - 1), 2 * k) if k else ():
                    if unit != LATE:
                        ssm_sums(n, unit)

            def ssm_sums(n, unit):
                u, t = UNITS[unit]
                c = u // UC
                o = head_sums(("so", c))
                wait_read(pe, n, ("ssm", unit // 2))
                if u % UC == 0 and t == 0:
                    if c == 0:
                        wait_read(pe, n, ("state",))
                    open_tile(n, ("so", c))
                    for s in range(2):
                        mm(o[:, s + 1], sqT[:, c, (s + 1) * P:(s + 2) * P], state[:, s, c, :, :].rearrange("p h e -> p (h e)"),
                           start=(s == 0), stop=False, skip_group_check=True)
                for i in range(2):
                    ins = mm(o[:, t, (2 * u + i) % HC, :], att[:, unit // 2 % NS, unit % 2, i, :], vs[:, t, 2 * u + i, :],
                             start=False, stop=True, skip_group_check=True)
                if u % UC == UC - 1 and t == T - 1:
                    ins.then_inc(fullsem(("so", c)), 1)

            def hidden(n, e, j):
                name = ("hid", e, j)
                o = open_tile(n, name)[:, 0:L]
                if e == NE:
                    ins = feature_major(o, xT[:, slot_xT(4)], wm1, slice(j * 128, (j + 1) * 128))
                else:
                    ins = feature_major(o, zT, w1[:, :, e], slice(j * 128, (j + 1) * 128))
                ins.then_inc(fullsem(name), 1)

            def second(n, e, j, k):
                if e == NE:
                    pe.wait_ge(blo_ready.sem, blo_ready.now(n, k + 1))
                    h16, w = bm16[:, k % NM], wm2[:, :, j * D:(j + 1) * D]
                else:
                    pe.wait_ge(lo_ready.sem, lo_ready.now(n, k + 1))
                    h16, w = hm16[:, k % NR], w2[:, :, e, j * D:(j + 1) * D]
                bias = bm2 if e == NE else bexp + e * D
                for pair, (t0, t1) in enumerate(PAIRS):
                    o = open_tile(n, ("ye", e, pair)) if j == 0 else at(("ye", e, pair))
                    for t in range(t0, t1):
                        if j == 0:
                            mm(o[0:P, (t - t0) * D:(t - t0 + 1) * D], ones[:, :], brow[:, bias:bias + D], start=(t == t0), stop=False,
                               skip_group_check=True)
                        for i, (a, b) in enumerate(((0, 0), (1, 0), (0, 1))):
                            ins = mm(o[0:P, (t - t0) * D:(t - t0 + 1) * D], h16[:, a, t * P:(t + 1) * P], w[:, b],
                                     start=False, stop=(j == NJ - 1 and i == 2), skip_group_check=True)
                    if j == NJ - 1:
                        ins.then_inc(fullsem(("ye", e, pair)), 1)

            def mlp(n, j):
                if j == 0:
                    wait_read(pe, n, ("xT", 4))
                    hidden(n, NE, 0)
                    return
                if j < NJ:
                    hidden(n, NE, j)
                if j >= LAGM:
                    second(n, NE, j - LAGM, j - LAGM)

            def moe(n, q):
                if q == 0:
                    wait_read(pe, n, ("xT", 5))
                if q < NE * NJ:
                    hidden(n, q // NJ, q % NJ)
                for k in seconds(q):
                    second(n, k // NJ, k % NJ, k)

            def gate_scores(n):
                wait_read(pe, n, ("xT", 5))
                o = open_tile(n, ("gate",))
                for t in range(T):
                    ins = token_major(o[0:P, t * NE:(t + 1) * NE], zT, t, wg, slice(0, NE), bgate, t == 0)
                ins.then_inc(fullsem(("gate",)), 1)

            nothing = lambda n, k=0: None
            pe.wait_ge(setup, NSETUP)
            pe.wait_ge(weights, 16 * NWEIGHTS)

            def between(name, k):
                if name == "patches":
                    pe.wait_ge(split_lo, NPB)
                    pe.wait_ge(bias_split, 2)
                if (name, k) == ("attend2", NU - 1):
                    pe.wait_ge(split_lo, len(all_pieces))

            run_schedule(dict(ssm_state=ssm_state, ssm=ssm, reduce=nothing, so_T=lambda n: transpose_split(n, 1),
                              so_out=lambda n: linear(n, "so2", 1, wsout, bsout), ao_T=lambda n: transpose_split(n, 2), patches=nothing,
                              proj=lambda n: linear(n, "sum", 2, wproj, bproj), sum_T=lambda n: transpose_split(n, 3),
                              out=lambda n: linear(n, "out", 3, wout, bout), norm3=nothing, norm3b=nothing, x2_T=lambda n: transpose_split(n, 4),
                              mlp=mlp, tokens=tokens, norm4=nothing, norm0=nothing, z=nothing, norm1=nothing,
                              z_T=lambda n: transpose_split(n, 5), gate=gate_scores, norm1b=nothing, 
                              x_T=lambda n: transpose_split(n, 0), qk=qk, values=values, scores=scores, attend0=attend0,
                              attend1=attend1, attend2=attend2, moe=moe), pe, between)

        @block.scalar
        def _(act):
            A = nc.scalar.activation

            def split_piece(k):
                _, n, (hi, _), _ = all_pieces[k]
                act.wait_ge(piece[k % 2], piece_count[k])
                A(hi, stage[k % 2][:, 0:n], ACT.Copy).then_inc(split_hi, 1)

            def evacuate(n, k):
                wait_full(act, n, ("xT", k))
                dst = zT[:, :, :] if k == 5 else xT[:, slot_xT(k)]
                A(dst.rearrange("p m l -> p (m l)"), at(("xT", k))[:, :].bitcast(fp16)[:, 0:3 * L], ACT.Copy).then_inc(readsem(("xT", k)), 1)

            def tokens(n):
                act.wait_ge(h0_done.sem, h0_done.before(n, 1))
                for t, m in ((0, P), (1, I1)):
                    wait_full(act, n, ("tok", t))
                    A(h0[0:m, t, :], at(("tok", t))[0:m, 0:D], ACT.Copy).then_inc(readsem(("tok", t)), 1)

            def qk(n, half):
                for m in range(4):
                    name = ("qk", 4 * half + m)
                    wait_full(act, n, name)
                    if half == 0:
                        dst = (qT, kT)[m // 2]
                        if m < 2:
                            A(dst[:, m, :], at(name)[0:DC, 0:L], ACT.Identity, scale=E ** -0.5, bias=bq4[:, m:m + 1]).then_inc(readsem(name), 1)
                        else:
                            A(dst[:, m - 2, :], at(name)[0:DC, 0:L], ACT.Identity, bias=bqk[:, m:m + 1]).then_inc(readsem(name), 1)
                    else:
                        act.wait_ge(elu_ready.sem, elu_ready.now(n, m - 1) if m >= 2 else elu_ready.before(n, 3 + m))
                        A(elue[:, m % 2, :], at(name)[0:DC, 0:L], ACT.Exp, bias=bqk[:, 4 + m:5 + m]).then_inc(elu_exp.sem, 1)

            def values(n):
                for t in range(T):
                    name = ("v", t)
                    wait_full(act, n, name)
                    o = at(name)[0:P, 0:2 * D].rearrange("p (a h e) -> p a h e", a=2, h=H)
                    A(va[:, t, :, 0:E], o[:, 0, :, :], ACT.Copy)
                    A(vs[:, t, :, 0:E], o[:, 1, :, :], ACT.Copy).then_inc(readsem(name), 1)

            def scores(n, u):
                for t in range(T):
                    k = u * T + t
                    w = P if t == 0 else W
                    act.wait_ge(nmax_ready.sem, nmax_ready.now(n, k + 1))
                    o = at(("score", k))[0:P, 0:2 * w].rearrange("p (i k) -> p i k", i=2)
                    for i in range(2):
                        ins = A(prob[:, u % 2, t, i, 2 * P - w:2 * P], o[:, i, :], ACT.Exp, bias=nmax[:, u % 2, t, i:i + 1])
                    ins.then_inc(readsem(("score", k)), 1)

            def ssm_state(n):
                wait_full(act, n, ("skt",))
                A(sktok[:, :, :].rearrange("p t d -> p (t d)"), at(("skt",))[0:P, 0:2 * D], ACT.Copy).then_inc(readsem(("skt",)), 1)

            def hidden(n, e, j, dst, dst16):
                name = ("hid", e, j)
                wait_full(act, n, name)
                A(dst, at(name)[:, 0:L], ACT.Gelu, bias=bh[:, e, j:j + 1])
                A(dst16, at(name)[:, 0:L], ACT.Gelu, bias=bh[:, e, j:j + 1]).then_inc(readsem(name), 1)

            def mlp(n, j):
                if j < NJ:
                    hidden(n, NE, j, bm[:, j % NM, :], bm16[:, j % NM, 0, :])

            def moe(n, q):
                if q < NE * NJ:
                    hidden(n, q // NJ, q % NJ, hm[:, q % NR, :], hm16[:, q % NR, 0, :])

            nothing = lambda n, k=0: None
            act.wait_ge(setup, NSETUP)
            act.wait_ge(weights, 16 * NWEIGHTS)
            act.wait_ge(bias_split, 2)
            for k in range(NPB):
                split_piece(k)
            todo = list(range(NPB, len(all_pieces)))

            def between(name, k):
                if name in ("scores", "attend0", "attend1"):
                    for _ in range(min(2, len(todo))):
                        split_piece(todo.pop(0))
                assert (name, k) != ("attend2", NU - 1) or not todo

            run_schedule(dict(ssm_state=ssm_state, ssm=nothing, reduce=nothing, so_T=lambda n: evacuate(n, 1), so_out=nothing,
                              ao_T=lambda n: evacuate(n, 2), patches=nothing, proj=nothing, sum_T=lambda n: evacuate(n, 3), out=nothing,
                              norm3=nothing, norm3b=nothing, x2_T=lambda n: evacuate(n, 4), mlp=mlp, tokens=tokens, norm4=nothing, norm0=nothing,
                              z=nothing, norm1=nothing, z_T=lambda n: evacuate(n, 5), gate=nothing, norm1b=nothing, 
                              x_T=lambda n: evacuate(n, 0), qk=qk, values=values, scores=scores, attend0=nothing, attend1=nothing,
                              attend2=nothing, moe=moe), act, between)

        @block.vector
        def _(dve):
            V = nc.vector
            links = {}

            def split_piece(k):
                kind, n, (hi, lo), _ = all_pieces[k]
                dve.wait_ge(split_hi, k + 1)
                r = slice(0, DB) if kind == "rest" else slice(0, 128)
                V.tensor_tensor(lo, stage[k % 2][r, 0:n], hi[r], ALU.subtract).then_inc(split_lo, 1)

            def link(n, part, ins):
                links[part] += 1
                ins.then_inc(part.sem, 1)
                dve.wait_ge(part.sem, part.now(n, links[part]))

            def linked(part):
                assert links[part] == part.per, (part.sem, links[part])

            def part_of_norm(k):
                return (first, first, second_part, second_part, gating)[k]

            def tile_of(name, pair):
                return (*name, pair) if isinstance(name, tuple) else (name, pair)

            def tok(name, pair):
                t0, t1 = PAIRS[pair]
                return at(tile_of(name, pair))[0:P, 0:(t1 - t0) * D].rearrange("p (t d) -> p t d", d=D)

            def moments(n, k, src):
                st, m, _ = moments_of(k)
                for t in range(T):
                    ins = V.bn_stats(st[:, t, :], src(t))
                link(n, part_of_norm(k), ins)
                hold(dve)
                for t in range(T):
                    ins = V.bn_aggr(m[:, t, :], st[:, t, :])
                ins.then_inc(var_ready.sem, 1)

            def scale(n, k, src, dst):
                _, m, r = moments_of(k)
                dve.wait_ge(rstd_ready.sem, rstd_ready.now(n, k + 1))
                for t in range(T):
                    ins = V.tensor_scalar(dst[:, t, :], src(t), m[:, t, 0:1], r[:, t:t + 1], ALU.subtract, ALU.mult)
                return ins

            def affine(n, k, buf):
                link(n, first if k == 0 else second_part,
                     V.tensor_tensor(buf[:, :, :], buf[:, :, :], lnw[:, k, 0:1, :].to_broadcast((P, T, D)), ALU.mult))
                return V.tensor_tensor(buf[:, :, :], buf[:, :, :], lnw[:, k, 1:2, :].to_broadcast((P, T, D)), ALU.add)

            def split(n, k, src):
                if k >= 1:
                    wait_full(dve, n, ("xT", k - 1))
                d = x16
                V.tensor_copy(d[:, :, 0:DA], src[:, :, 0:DA])
                link(n, (first, second_part, second_part, second_part, second_part, gating)[k], V.tensor_copy(d[:, :, 2 * DA:2 * DA + DB], src[:, :, DA:D]))
                V.tensor_tensor(d[:, :, DA:2 * DA], src[:, :, 0:DA], d[:, :, 0:DA], ALU.subtract)
                V.tensor_tensor(d[:, :, 2 * DA + DB:2 * D], src[:, :, DA:D], d[:, :, 2 * DA:2 * DA + DB], ALU.subtract)\
                    .then_inc(x16_ready.sem, 1)

            def of(buf):
                return lambda t: buf[:, t, :]

            def reduce(n, h):
                dve.wait_ge(x_loaded[h % 2].sem, x_loaded[h % 2].now(n, 16 * (h // 2 + 1)))
                V.tensor_reduce(pooled[:, h, :], xin[:, h % 2, :].rearrange("p (r j w) -> p j r w", j=NP, w=KP),
                                axis=AX.XY, op=ALU.add).then_inc(x_read.sem, 1)

            def patches(n):
                links[first] = 0
                dve.wait_ge(x_read.sem, x_read.now(n, 6))
                link(n, first, V.tensor_tensor(pooled[:, 0:3, :], pooled[:, 0:3, :], pooled[:, 3:6, :], ALU.add))
                for g in range(3):
                    V.tensor_tensor(patch[:, g, :, :], pooled[:, g, None, :].to_broadcast((PX, NP, NP)),
                                    patchm[:, :, None].to_broadcast((PX, NP, NP)), ALU.mult).then_inc(patch_ready.sem, 1)

            def norm0(n):
                for t in range(2):
                    wait_read(dve, n, ("tok", t))
                dve.wait_ge(txt_loaded.sem, txt_loaded.now(n, 32))
                moments(n, 0, of(h0))

            def norm1(n):
                link(n, first, scale(n, 0, of(h0), y))
                moments(n, 1, of(y))

            def norm1b(n):
                link(n, first, scale(n, 1, of(y), xn))
                link(n, first, affine(n, 0, xn))
                split(n, 0, xn)

            def qk(n, half):
                for m in range(4 * half):
                    name = ("qk", 4 + m)
                    dve.wait_ge(elu_exp.sem, elu_exp.now(n, m + 1))
                    V.tensor_scalar(elur[:, m % 2, :], at(name)[0:DC, 0:L], bneg[:, m:m + 1], bpos[:, m:m + 1],
                                    ALU.max, ALU.add).then_inc(readsem(name), 1)
                    wait_read(dve, n, name)
                    if m == 0:
                        dve.wait_ge(hX_ready.sem, hX_ready.before(n, 2 * NU))
                    V.scalar_tensor_tensor((sqT, skT)[m // 2][:, m % 2, :], elue[:, m % 2, :], 1.0, elur[:, m % 2, :],
                                           ALU.min, ALU.add).then_inc(elu_ready.sem, 1)

            def scores(n, u):
                for t in range(T):
                    k = u * T + t
                    w = P if t == 0 else W
                    wait_full(dve, n, ("score", k))
                    V.tensor_reduce(nmax[:, u % 2, t, :], at(("score", k))[0:P, 0:2 * w].rearrange("p (i k) -> p i k", i=2),
                                    axis=AX.X, op=ALU.max, negate=True).then_inc(nmax_ready.sem, 1)

            def weights_T(n, k):
                if k == 0:
                    dve.wait_ge(elu_ready.sem, elu_ready.now(n, 4))
                wait_full(dve, n, ("probT", k))
                c0 = 1 if k % T == 0 else 0
                o = at(("probT", k))[0:P, 0:4 * P].rearrange("p (i c q) -> p i c q", i=2, c=2)
                V.tensor_copy(probT[:, k % 2, :, c0:2, :], o[:, :, c0:2, :]).then_inc(readsem(("probT", k)), 1)

            def attend0(n, u):
                weights_T(n, u * T)
                weights_T(n, u * T + 1)

            def attend1(n, u):
                weights_T(n, u * T + 2)

            def attend2(n, u):
                if u % UC == UC - 1:
                    normalise(n, ("ao", u // UC), 0.0, ao)
                if u == NU - 1:
                    linked(first)

            def normalise(n, name, eps, dst):
                c = name[1]
                wait_full(dve, n, name)
                o = at(name)[0:P, 0:T * HC * (E + 1)].rearrange("p (t h e) -> p t h e", t=T, h=HC)
                part = first if name[0] == "ao" else second_part
                link(n, part, V.tensor_scalar(den[:, :, :], o[:, :, :, E], eps, None, ALU.add))
                link(n, part, V.reciprocal(den[:, :, :], den[:, :, :]))
                V.tensor_tensor(dst[:, :, c * HC:(c + 1) * HC, :], o[:, :, :, 0:E], den[:, :, :, None].to_broadcast((P, T, HC, E)),
                                ALU.mult).then_inc(readsem(name), 1)

            def ssm_state(n):
                links[second_part] = 0
                wait_full(dve, n, ("state",))
                V.tensor_tensor(state[:, :, :, :, :].rearrange("p t c h e -> p (t c) h e"),
                                at(("state",))[0:DC, 0:4 * HC * (E + 1)].rearrange("p (m h e) -> p m h e", m=4, h=HC),
                                headm[:, None, :, None].to_broadcast((DC, 4, HC, E + 1)), ALU.mult).then_inc(readsem(("state",)), 1)

            def ssm(n, k):
                if k < NSJ:
                    wait_full(dve, n, ("ssm", k))
                    V.tensor_tensor(att[:, k % NS].rearrange("p m i q -> p (m i) q"), at(("ssm", k))[0:P, 0:4 * P].rearrange("p (m q) -> p m q", m=4),
                                    causal[:, None, :].to_broadcast((P, 4, P)), ALU.mult).then_inc(readsem(("ssm", k)), 1)
                if k in (NSJ // 2 + 1, NSJ):
                    normalise(n, ("so", k // NSJ), 1e-4 * E ** 0.5, so)

            flat = lambda b: b[:, :, :, :].rearrange("p t h e -> p t (h e)")

            def so_T(n):
                wait_read(dve, n, ("so", 1))
                split(n, 1, flat(so))
                split(n, 2, flat(ao))

            def so_tile(t):
                return tok("so2", t // 2)[:, t % 2, :]

            def so_out(n):
                for pair in range(2):
                    wait_full(dve, n, ("so2", pair))
                moments(n, 2, so_tile)

            def ao_T(n):
                dve.wait_ge(rstd_ready.sem, rstd_ready.now(n, 3))
                for t in range(T):
                    ins = V.tensor_scalar(so2[:, t, :], so_tile(t), mv[:, t, 0:1], rstd[:, t:t + 1], ALU.subtract, ALU.mult)
                    if t > 0:
                        ins.then_inc(readsem(("so2", t - 1)), 1)
                wait_read(dve, n, ("so2", 0))
                wait_read(dve, n, ("so2", 1))
                link(n, second_part, affine(n, 1, so2))

            def add_pairs(n, name, dst, other):
                for pair, (t0, t1) in enumerate(PAIRS):
                    tile = tile_of(name, pair)
                    wait_full(dve, n, tile)
                    V.tensor_tensor(dst[:, t0:t1, :], tok(name, pair), other[:, t0:t1, :], ALU.add).then_inc(readsem(tile), 1)
                for pair in range(2):
                    wait_read(dve, n, tile_of(name, pair))

            def proj(n):
                add_pairs(n, "sum", so2, so2)
                split(n, 3, so2)

            def out_(n):
                add_pairs(n, "out", hx, y)
                moments(n, 3, of(hx))

            def norm3(n):
                link(n, second_part, scale(n, 3, of(hx), xn))
                link(n, second_part, affine(n, 2, xn))

            def norm3b(n):
                split(n, 4, xn)

            def mlp(n, j):
                if j < NJ:
                    wait_read(dve, n, ("hid", NE, j))
                    V.tensor_tensor(bm16[:, j % NM, 1, :], bm[:, j % NM, :], bm16[:, j % NM, 0, :], ALU.subtract).then_inc(blo_ready.sem, 1)
                if j == NJ + LAGM - 1:
                    dve.wait_ge(h0_done.sem, h0_done.now(n, 1))
                    add_pairs(n, ("ye", NE), hx, hx)
                    linked(second_part)

            def norm4(n):
                links[gating] = 0
                moments(n, 4, of(hx))

            def z(n):
                link(n, gating, scale(n, 4, of(hx), xn))
                split(n, 5, xn)

            def gate_scores(n):
                wait_full(dve, n, ("gate",))
                V.tensor_copy(gate[:, :, :], at(("gate",))[0:P, 0:T * NE].rearrange("p (t e) -> p t e", t=T)).then_inc(readsem(("gate",)), 1)
                wait_read(dve, n, ("gate",))
                hold(dve)
                for t in range(T):
                    ins = V.max(top8[:, t, :], gate[:, t, :])
                link(n, gating, ins)
                hold(dve)
                for t in range(T):
                    ins = V.max_index(idx8[:, t, :], top8[:, t, :], gate[:, t, :])
                link(n, gating, ins)
                link(n, gating, V.tensor_copy(idxf[:, :, :], idx8[:, :, :]))
                for t in range(T):
                    V.tensor_scalar(comb[:, t, :], iota8[:, :], idxf[:, t, 0:1], top8[:, t, 0:1], ALU.is_equal, ALU.mult)
                    ins = V.tensor_scalar(comb2[:, t, :], iota8[:, :], idxf[:, t, 1:2], top8[:, t, 1:2], ALU.is_equal, ALU.mult)
                link(n, gating, ins)
                V.tensor_tensor(comb[:, :, :], comb[:, :, :], comb2[:, :, :], ALU.add).then_inc(comb_ready.sem, 1)
                linked(gating)

            def moe(n, q):
                if 1 <= q <= NE * NJ:
                    k = q - 1
                    wait_read(dve, n, ("hid", k // NJ, k % NJ))
                    V.tensor_tensor(hm16[:, k % NR, 1, :], hm[:, k % NR, :], hm16[:, k % NR, 0, :], ALU.subtract).then_inc(lo_ready.sem, 1)
                for k in seconds(q):
                    if k % NJ == NJ - 1:
                        add_expert(n, k // NJ)

            def add_expert(n, e):
                if e == 0:
                    dve.wait_ge(stored.sem, stored.before(n, 16))
                for pair, (t0, t1) in enumerate(PAIRS):
                    name = ("ye", e, pair)
                    wait_full(dve, n, name)
                    if e:
                        wait_read(dve, n, ("ye", e - 1, pair))
                    for t in range(t0, t1):
                        ins = V.scalar_tensor_tensor(hres[:, t, :], at(name)[0:P, (t - t0) * D:(t - t0 + 1) * D], comb[:, t, e:e + 1],
                                                     (hres if e else hx)[:, t, :], ALU.mult, ALU.add)
                    ins.then_inc(readsem(name), 1)

            nothing = lambda n, k=0: None
            dve.wait_ge(weights, 16 * NWEIGHTS)
            V.tensor_scalar(bq4[:, :], bqk[:, 0:2], E ** -0.5, None, ALU.mult)
            V.tensor_scalar(bneg[:, :], bqk[:, 4:8], -1.0, None, ALU.mult)
            V.tensor_scalar(bpos[:, :], bqk[:, 4:8], 1e-4, None, ALU.add)
            V.memset(brow[:, :], 0.0).then_inc(bias_split, 1)
            dve.wait_ge(bias_split, 1)
            parts = ((brow32, slice(0, bgate)), (bg32, slice(bgate, bexp)), (bexp32, slice(bexp, NBR)))
            for b32, c in parts:
                V.tensor_copy(brow[0:1, c], b32[0:1, :])
                V.tensor_copy(brow[32:33, c], b32[32:33, :]).then_inc(bias_hi, 1)
            dve.wait_ge(bias_hi, len(parts))
            for b32, c in parts:
                ins = V.tensor_tensor(brow[32:33, c], b32[32:33, :], brow[32:33, c], ALU.subtract)
            ins.then_inc(bias_split, 1)
            dve.wait_ge(setup, NSETUP)
            for k in range(NPB):
                split_piece(k)
            todo = list(range(NPB, len(all_pieces)))

            def between(name, k):
                if name in ("scores", "attend0", "attend1"):
                    for _ in range(min(2, len(todo))):
                        split_piece(todo.pop(0))
                assert (name, k) != ("attend2", NU - 1) or not todo

            run_schedule(dict(ssm_state=ssm_state, ssm=ssm, reduce=reduce, so_T=so_T, so_out=so_out, ao_T=ao_T, patches=patches,
                              proj=proj, sum_T=nothing, out=out_, norm3=norm3, norm3b=norm3b, x2_T=nothing, mlp=mlp, tokens=nothing, norm4=norm4,
                              norm0=norm0, z=z, norm1=norm1, z_T=nothing, gate=gate_scores, norm1b=norm1b, 
                              x_T=nothing, qk=qk, values=nothing, scores=scores, attend0=attend0, attend1=attend1, attend2=attend2,
                              moe=moe), dve, between)


_INS = ['x', 'txt', 'L0_tok_channel_weights', 'L0_attn_ln1_g', 'L0_attn_ln1_b', 'L0_attn_attn_qkv_w', 'L0_attn_attn_qkv_b',
        'L0_attn_attn_proj_w', 'L0_attn_attn_proj_b', 'L0_attn_ssm_qkv_w', 'L0_attn_ssm_qkv_b', 'L0_attn_ssm_out_w',
        'L0_attn_ssm_out_b', 'L0_attn_ssm_ln_g', 'L0_attn_ssm_ln_b', 'L0_attn_out_w', 'L0_attn_out_b', 'L0_attn_mlp_w1',
        'L0_attn_mlp_b1', 'L0_attn_mlp_w2', 'L0_attn_mlp_b2', 'L0_attn_lnm_g', 'L0_attn_lnm_b',
        'L0_ffn_Wg', 'L0_ffn_bg', 'L0_ffn_W1', 'L0_ffn_b1', 'L0_ffn_W2', 'L0_ffn_b2']
_OUTS = [((16, 324, 192), 'float32')]


def kernel(**inputs):
    import numpy as _np
    import concourse.bacc as _bacc
    from concourse import mybir as _mybir
    from concourse.bass_utils import run_bass_kernel_spmd as _run

    nc = _bacc.Bacc("TRN2", target_bir_lowering=False, num_devices=1)
    arrays, args = {}, []
    for name in _INS:
        a = _np.ascontiguousarray(inputs[name])
        arrays[f"in_{name}_dram"] = a
        args.append(nc.dram_tensor(f"in_{name}_dram", a.shape, _mybir.dt.from_np(a.dtype), kind="ExternalInput").ap())
    for i, (shape, dtype) in enumerate(_OUTS):
        dt = _mybir.dt.from_np(_np.dtype(dtype))
        args.append(nc.dram_tensor(f"out_{i}_dram", shape, dt, kind="ExternalOutput").ap())
    early_fusion_moe_kernel(nc, *args)
    r = _run(nc, [arrays], core_ids=[0])
    return r.results[0]["out_0_dram"]
```

```python
import concourse.bass as bass
from concourse import mybir
from contextlib import ExitStack


def early_fusion_moe_kernel(nc, x, txt, cw, ln1_g, ln1_b, qkv_w, qkv_b, proj_w, proj_b,
                            sqkv_w, sqkv_b, sout_w, sout_b, sln_g, sln_b, out_w, out_b,
                            mlp_w1, mlp_b1, mlp_w2, mlp_b2, lnm_g, lnm_b,
                            Wg, bg, W1, b1, W2, b2, out):
    fp32 = mybir.dt.float32
    fp16 = mybir.dt.float16
    bf16 = mybir.dt.bfloat16
    u32 = mybir.dt.uint32
    ALU = mybir.AluOpType
    ACT = mybir.ActivationFunctionType
    AX = mybir.AxisListType

    S, C, IMG, _ = x.shape
    D = cw.shape[1]
    KP = 16
    NP = IMG // KP
    IT = NP * NP
    TX = txt.shape[1]
    L = IT + TX
    T = 3
    P = L // T
    I1 = IT - P
    H = 12
    E = D // H
    HC = H // 2
    NU = H // 2
    WIN = 64
    W = P + WIN - 1
    DC = D // 2
    DA = 128
    DB = D - DA
    HID = mlp_w1.shape[1]
    NJ = HID // 128
    NE = Wg.shape[1]
    GC = C // 3
    PX = GC * NP * 2
    RW = IMG * KP // 2
    EPS = 1e-5
    FAR = -1e9


    ctx = ExitStack()
    with ctx:
        def sb(name, shape, dt=fp32):
            return ctx.enter_context(nc.sbuf_tensor(name, shape, dt))

        def sem(name):
            return ctx.enter_context(nc.semaphore(name))

        cwrep = sb("cwrep", [PX, 3, D])
        wqkv = sb("wqkv", [128, 4, 2, 3 * D], fp16)
        wproj = sb("wproj", [128, 4, D], fp16)
        wsout = sb("wsout", [128, 4, D], fp16)
        wout = sb("wout", [128, 4, D], fp16)
        wm1 = sb("wm1", [128, 4, HID], fp16)
        wm2 = sb("wm2", [128, 2, NJ * D], fp16)
        wg = sb("wg", [128, 4, NE], fp16)
        w1 = sb("w1", [128, 4, NE, HID], fp16)
        w2 = sb("w2", [128, 2, NE, NJ * D], fp16)
        bv, bproj, bsout, bout, bm2 = 0, 2 * D, 3 * D, 4 * D, 5 * D
        bgate = 6 * D
        bexp = 6 * D + NE
        NBR = bexp + NE * D
        brow = sb("brow", [33, NBR], fp16)
        ones = sb("ones", [33, P], fp16)
        bqk = sb("bqk", [DC, 8])
        bq4 = sb("bq4", [DC, 2])
        bneg = sb("bneg", [DC, 4])
        bpos = sb("bpos", [DC, 4])
        bh = sb("bh", [128, NE + 1, NJ])
        lnw = sb("lnw", [P, 3, 2, D])
        ident = sb("ident", [128, 128])
        ident16 = sb("ident16", [128, 128], fp16)
        identb = sb("identb", [128, 128], bf16)
        band = sb("band", [P, W], bf16)
        causal = sb("causal", [P, P])
        headm = sb("headm", [DC, HC])
        patchm = sb("patchm", [PX, NP])
        iota8 = sb("iota8", [P, NE])
        mhalf = sb("mhalf", [P, T])

        xin = sb("xin", [PX, 2, RW // 2])
        pooled = sb("pooled", [PX, 6, NP])
        shared = sb("shared", [PX, 8 * P])
        patch = shared[:, 0:3 * IT].rearrange("p (g i j) -> p g i j", g=3, i=NP)
        elur = shared[0:DC, 0:2 * L].rearrange("p (m l) -> p m l", m=2)
        probT = shared[0:P, :].rearrange("p (m i c q) -> p m i c q", m=2, i=2, c=2)
        h0 = sb("h0", [P, T, D])
        y = sb("y", [P, T, D])
        hx = sb("hx", [P, T, D])
        xn = sb("xn", [P, T, D])
        stats = sb("stats", [P, T, 6])
        mv = sb("mv", [P, T, 2])
        rstd = sb("rstd", [P, T])
        unused = sb("unused", [1, 1])
        stats4, mv4, rstd4 = sb("stats4", [P, T, 6]), sb("mv4", [P, T, 2]), sb("rstd4", [P, T])
        x16 = sb("x16", [P, T, 2 * D], fp16)
        xT = sb("xT", [128, 2, 3, L], fp16)
        zT = sb("zT", [128, 3, L], fp16)
        qT = sb("qT", [DC, 2, L])
        kT = sb("kT", [DC, 2, L])
        sqT = sb("sqT", [DC, 2, L])
        skT = sb("skT", [DC, 2, L])
        NX = 3
        hX = sb("hX", [DC, NX, 2, L])
        va = sb("va", [P, T, H, E + 1])
        vs = sb("vs", [P, T, H, E + 1])
        nmax = sb("nmax", [P, 2, T, 2])
        prob = sb("prob", [P, 2, T, 2, 2 * P])
        state = sb("state", [DC, 2, 2, HC, E + 1])
        NS = 2
        att = shared[0:P, :].rearrange("p (k m i q) -> p k m i q", k=NS, m=2, i=2)
        den = sb("den", [P, T, HC])
        both = sb("both", [P, 2 * T * D])
        ao, so = (both[:, m * T * D:(m + 1) * T * D].rearrange("p (t h e) -> p t h e", t=T, h=H) for m in range(2))
        sktok = both[:, T * D:T * D + 2 * D].rearrange("p (t d) -> p t d", t=2)
        elue = both[0:DC, 0:2 * L].rearrange("p (m l) -> p m l", m=2)
        brow32 = both[0:33, 0:6 * D]
        bg32 = sb("bg32", [33, NE])
        bexp32 = hX[0:33].rearrange("p x i l -> p (x i l)")[:, 0:NE * D]
        so2 = xn
        NR = 4
        hm = sb("hm", [128, NR, L])
        hm16 = sb("hm16", [128, NR, 2, L], fp16)
        NM = 2
        bm = sb("bm", [128, NM, L])
        bm16 = sb("bm16", [128, NM, 2, L], fp16)
        stage = [hm[:, :, :].rearrange("p r l -> p (r l)"), hm16[:, :, :, :].rearrange("p r m l -> p (r m l)").bitcast(fp32),
                 bm[:, :, :].rearrange("p r l -> p (r l)"), bm16[:, :, :, :].rearrange("p r m l -> p (r m l)").bitcast(fp32)]
        hres = sb("hres", [P, T, D])
        gate = sb("gate", [P, T, NE])
        top8 = sb("top8", [P, T, 8])
        idx8 = sb("idx8", [P, T, 8], u32)
        idxf = sb("idxf", [P, T, 8])
        comb = sb("comb", [P, T, NE])
        comb2 = sb("comb2", [P, T, NE])

        bank = [ctx.enter_context(nc.psum_tensor(f"bank{i}", [128, 512], fp32)) for i in range(8)]

        ring_a, acc_a, ring_h, ring_y = (0, 1, 2), 7, (3, 4), (5, 6)
        PAIRS = ((0, 2), (2, 3))
        UNITS = [(u, t) for u in range(NU) for t in range(T)]
        NSJ = len(UNITS) // 2
        UC = NU // 2
        AO_AT = 4
        LATE = NSJ
        LAG, LAGM = NR - 1, NM - 1
        place, turn = {}, [0] * 8

        def plan(name, b):
            place[name] = (b, turn[b])
            turn[b] += 1

        ring = [0]

        def plan_a(*names):
            for name in names:
                plan(name, ring_a[ring[0] % 3])
                ring[0] += 1

        plan_a(("tok", 0), ("tok", 1), ("xT", 0))
        plan_a(*[("qk", m) for m in range(4)])
        plan_a(*[("v", t) for t in range(T)])
        plan_a(*[("qk", m) for m in range(4, 8)])
        for c in range(2):
            plan(("ao", c), acc_a)
        for u in range(NU + 1):
            if u < NU:
                plan_a(*[("score", u * T + t) for t in range(T)])
            if u > 0:
                plan_a(*[("probT", (u - 1) * T + t) for t in range(T)])
        plan_a(("skt",), ("state",))
        plan_a(*[("ssm", k) for k in range(AO_AT)], ("xT", 1), *[("ssm", k) for k in range(AO_AT, NSJ)])
        for c in range(2):
            plan(("so", c), acc_a)
        plan_a(("xT", 2), ("so2", 0), ("so2", 1), ("sum", 0), ("sum", 1), ("xT", 3), ("out", 0), ("out", 1), ("xT", 4))
        for j in range(NJ):
            plan(("hid", NE, j), ring_a[j % 2])
        plan(("ye", NE, 0), acc_a)
        plan(("ye", NE, 1), ring_a[2])
        for name in (("xT", 5), ("gate",)):
            plan(name, acc_a)
        for e in range(NE):
            for j in range(NJ):
                plan(("hid", e, j), ring_h[j % 2])
            for pair in range(2):
                plan(("ye", e, pair), ring_y[pair])

        class Count:
            def __init__(self, name, per):
                self.sem, self.per = sem(name), per
                counts.append(self)

            def now(self, n, k):
                return n * self.per + (self.per + k)

            def before(self, n, k):
                return n * self.per + k

        counts = []
        full = [Count(f"bank{b}_full", turn[b]) for b in range(8)]
        read = [Count(f"bank{b}_read", turn[b]) for b in range(8)]

        def wait_full(eng, n, name):
            b, k = place[name]
            eng.wait_ge(full[b].sem, full[b].now(n, k + 1))

        def wait_read(eng, n, name):
            b, k = place[name]
            eng.wait_ge(read[b].sem, read[b].now(n, k + 1))

        def wait_free(eng, n, name):
            b, k = place[name]
            eng.wait_ge(read[b].sem, read[b].now(n, k) if k else read[b].before(n, turn[b]))

        def at(name):
            return bank[place[name][0]]

        def fullsem(name):
            return full[place[name][0]].sem

        def readsem(name):
            return read[place[name][0]].sem

        NQ = NE * NJ + LAG - 1

        def seconds(q):
            return [k for k in (q - LAG, q - LAG + 1) if 0 <= k < NE * NJ and (k % NJ == NJ - 1) == (k == q - LAG + 1)]

        NSETUP = 28
        FIRST_LINKS, BLOCK_LINKS, GATE_LINKS = 11, 13, 4
        STEPS = [
            ("ssm_state", None, 1, 1), ("ssm", 0, 1, 1), ("reduce", 0, 0, 0), ("ssm", 1, 1, 1), ("reduce", 1, 0, 0),
            ("ssm", 2, 1, 1), ("ao_split", None, 1, 0), ("ssm", 3, 1, 1), ("ao_T", None, 1, 0), ("reduce", 2, 0, 0),
            ("ssm", 4, 1, 1), ("reduce", 3, 0, 0), ("reduce", 4, 0, 0), ("ssm", 5, 1, 1), ("reduce", 5, 0, 0),
            ("ssm", 6, 1, 1), ("ssm", 7, 1, 0), ("ssm", 8, 1, 1), ("ssm", 9, 1, 2),
            ("so_T", None, 1, 1), ("so_out", None, 1, 1), ("norm2", None, 1, 1), ("proj", None, 1, 3),
            ("sum_T", None, 1, 1), ("patches", None, 0, 0), ("out", None, 1, 1), ("norm3", None, 1, 1),
            ("norm3b", None, 1, 2), ("x2_T", None, 1, 1),
            ("mlp", 0, 1, 1), ("mlp", 1, 1, 0), ("mlp", 2, 1, 0), ("mlp", 3, 1, 1), ("mlp", 4, 1, 0), ("mlp", 5, 1, 0),
            ("mlp", 6, 1, 0), ("norm4", None, 1, 1), ("tokens", None, 0, 2), ("z", None, 1, 2), ("norm0", None, 0, 0),
            ("z_T", None, 1, 2), ("norm1", None, 0, 0), ("gate", None, 1, 3), ("norm1b", None, 0, 2),
            ("x_T", None, 0, 1), ("qk", 0, 0, 1), ("values", None, 0, 0), ("qk", 1, 0, 0),
            ("scores", 0, 0, 0), ("scores", 1, 0, 1), ("attend0", 0, 0, 1), ("attend1", 0, 0, 2), ("attend2", 0, 0, 0),
            ("scores", 2, 0, 0), ("attend0", 1, 0, 1), ("attend1", 1, 0, 0), ("attend2", 1, 0, 0), ("scores", 3, 0, 1),
            ("attend0", 2, 0, 1), ("attend1", 2, 0, 0), ("attend2", 2, 0, 0), ("scores", 4, 0, 1), ("attend0", 3, 0, 1),
            ("attend1", 3, 0, 0), ("attend2", 3, 0, 0), ("scores", 5, 0, 1), ("attend0", 4, 0, 1), ("attend1", 4, 0, 0),
            ("attend2", 4, 0, 0), ("attend0", 5, 0, 1), ("attend1", 5, 0, 0), ("attend2", 5, 0, 0),
        ]
        at_gate = [name for name, *_ in STEPS].index("gate")
        QA = sum(moe for *_, moe in STEPS[at_gate:])

        def run_schedule(stage, eng, between=None):
            def turn(i):
                def now(behind):
                    return not isinstance(i, int) or 0 <= i - behind < S

                behind, q = 2, QA
                for at_step, (name, k, b, moe) in enumerate(STEPS):
                    if now(b):
                        if k is None:
                            stage[name](i - b if b else i)
                        else:
                            stage[name](i - b if b else i, k)
                        if isinstance(i, int) and i <= 1 and between:
                            between(i, name, k)
                    if name == "gate":
                        assert q >= NQ, "the experts of sample i - 2 are through"
                        behind, q = 1, 0
                    for _ in range(moe):
                        if now(behind) and q < NQ:
                            stage["moe"](i - behind, q)
                        q += 1

            turn(0)
            turn(1)
            with eng.Fori(2, S) as i:
                turn(i)
            turn(S)
            turn(S + 1)

        setup = sem("setup")
        weights = sem("weights")
        cw_loaded = sem("cw_loaded")
        split_hi = sem("split_hi")
        split_lo = sem("split_lo")
        piece = [sem(f"piece{i}") for i in range(4)]
        bias_cols = sem("bias_cols")
        bias_lo = sem("bias_lo")
        bias_hi = sem("bias_hi")
        x_loaded = [Count(f"x_loaded{h}", 48) for h in range(2)]
        x_read = Count("x_read", 6)
        txt_loaded = Count("txt_loaded", 32)
        h0_done = Count("h0_done", 1)
        patch_ready = Count("patch_ready", 3)
        var_ready = Count("var_ready", 5)
        eps_added = Count("eps_added", 5)
        rstd_ready = Count("rstd_ready", 5)
        x16_ready = Count("x16_ready", 6)
        elu_exp = Count("elu_exp", 4)
        elu_ready = Count("elu_ready", 4)
        hX_ready = Count("hX_ready", 2 * NU)
        nmax_ready = Count("nmax_ready", len(UNITS))
        lo_ready = Count("lo_ready", NE * NJ)
        blo_ready = Count("blo_ready", NJ)
        top_ready = Count("top_ready", 1)
        comb_ready = Count("comb_ready", 3)
        stored = Count("stored", 16)
        first, second_part, gating = Count("first", FIRST_LINKS), Count("second_part", BLOCK_LINKS), Count("gating", GATE_LINKS)
        held = sem("held")

        def moments_of(k):
            return (stats4, mv4, rstd4) if k == 4 else (stats, mv, rstd)

        def slot_xT(k):
            return (1, 0, 1, 0, 0)[k]

        def hold(eng):
            eng.sem_inc(held, 1)

        def pieces():
            def width(dst, src, n):
                yield "wide", n, (dst[:, 0], dst[:, 1]), [(slice(0, 128), src[0:DA])]
                yield "rest", n, (dst[:, 2], dst[0:DB, 3]), [(slice(0, DB), src[DA:D]), (slice(DB, 128), src[DA:D])]

            yield from width(wqkv[:, :, 0], qkv_w, 3 * D)
            yield from width(wqkv[:, :, 1], sqkv_w, 3 * D)
            yield from width(wsout, sout_w, D)
            yield from width(wproj, proj_w, D)
            yield from width(wm1, mlp_w1, HID)
            yield from width(wout, out_w, D)
            yield from width(wg, Wg, NE)
            for half in range(2):
                j = slice(half * NJ // 2 * D, (half + 1) * NJ // 2 * D)
                yield "rows", NJ // 2 * D, (wm2[:, 0, j], wm2[:, 1, j]), [(slice(0, 128), rows(mlp_w2, half))]

        def pieces_after(i, name):
            if i == 0:
                return dict(patches=1, norm0=1, norm1=2, qk=1, scores=1, attend0=2, attend1=2, attend2=2).get(name, 0)
            return 0

        def expert_pieces(e):
            yield "wide", HID, (w1[:, 0, e], w1[:, 1, e]), [(slice(0, 128), W1[e, 0:DA])]
            yield "rest", HID, (w1[:, 2, e], w1[0:DB, 3, e]), [(slice(0, DB), W1[e, DA:D]), (slice(DB, 128), W1[e, DA:D])]
            for half in range(2):
                j = slice(half * NJ // 2 * D, (half + 1) * NJ // 2 * D)
                yield "rows", NJ // 2 * D, (w2[:, 0, e, j], w2[:, 1, e, j]), [(slice(0, 128), rows(W2[e], half))]

        def rows(w, half):
            n = HID // 2
            return w[half * n:(half + 1) * n, :].rearrange("(j p) d -> p j d", p=128)

        block_pieces = list(pieces())
        NPB = 4
        all_pieces = block_pieces + [p for e in range(NE) for p in expert_pieces(e)]
        NSLOT = len(stage)
        landed = [0] * NSLOT
        piece_count = []
        for k, (_, _, _, srcs) in enumerate(all_pieces):
            landed[k % NSLOT] += 16 * len(srcs)
            piece_count.append(landed[k % NSLOT])

        block = ctx.enter_context(nc.Block())

        @block.sync
        def _(sp):
            def load_piece(k):
                _, n, _, srcs = all_pieces[k]
                if k >= NSLOT:
                    sp.wait_ge(split_lo, k - NSLOT + 1)
                for part, src in srcs:
                    d = stage[k % NSLOT][part, 0:n]
                    if len(src.shape) == 3:
                        d = d.rearrange("p (j d) -> p j d", d=D)
                    sp.dma_start(d, src).then_inc(piece[k % NSLOT], 16)

            x_v = x.rearrange("s (g c) (i b u r) w -> s u g (c i b) (r w)", g=3, i=NP, b=2, u=2)

            def load_x(n, h, lead):
                sp.wait_ge(x_read.sem, lead[h])
                sp.dma_start(xin[:, h % 2, :], x_v[bass.ds(n, 1), h // 3, h % 3, :, :].rearrange("s p f -> (s p) f"))\
                    .then_inc(x_loaded[h % 2].sem, 16)

            def load_text(n, lead):
                sp.wait_ge(h0_done.sem, lead[6])
                sp.dma_start(h0[I1:P, 1, :], txt[bass.ds(n, 1), 0:P - I1, :].rearrange("s p d -> (s p) d")).then_inc(txt_loaded.sem, 16)
                sp.dma_start(h0[:, 2, :], txt[bass.ds(n, 1), P - I1:TX, :].rearrange("s p d -> (s p) d")).then_inc(txt_loaded.sem, 16)

            def load_sample(n, lead):
                for h in range(6):
                    load_x(n, h, lead)
                load_text(n, lead)

            def store_sample(n, lead):
                for b, v in zip(ring_y, lead):
                    sp.wait_ge(read[b].sem, v)
                sp.dma_start(out[bass.ds(n, 1), :, :].rearrange("s (t p) d -> p (s t) d", t=T), hres[:, :, :]).then_inc(stored.sem, 16)

            def leads(n):
                return [x_read.before(n, 5), x_read.before(n, 6)] + [x_read.now(n, h - 1) for h in range(2, 6)] + [h0_done.before(n, 1)]

            for h in range(2):
                load_x(0, h, leads(0))
            for g in range(3):
                for c in range(GC):
                    sp.dma_start(cwrep[c * 2 * NP:(c + 1) * 2 * NP, g, :], cw[g * GC + c:g * GC + c + 1, :].to_broadcast((2 * NP, D)))\
                        .then_inc(cw_loaded, 16)
                if g == 0:
                    load_piece(0)
                    load_piece(1)
                load_x(0, 2 + g, leads(0))
            load_x(0, 5, leads(0))
            load_text(0, leads(0))
            for k in range(2, len(all_pieces)):
                load_piece(k)
            load_sample(1, leads(1))
            with sp.Fori(2, S) as i:
                load_sample(i, [sp.snap(v) for v in leads(i)])
                store_sample(i - 2, [sp.snap(read[b].now(i - 2, turn[b])) for b in ring_y])
            for n in (S - 2, S - 1):
                store_sample(n, [read[b].now(n, turn[b]) for b in ring_y])
            sp.wait_ge(stored.sem, stored.now(S - 1, 16))

        NWEIGHTS = 16 + 6 + 4

        @block.gpsimd
        def _(pool):
            steps = [0]

            def step(ins):
                steps[0] += 1
                ins.then_inc(setup, 1)
                pool.wait_ge(setup, steps[0])

            for c in counts:
                pool.sem_inc(c.sem, c.per)
            step(pool.memset(patchm[:, :], 0.0))
            for c in range(GC):
                for b in range(2):
                    step(pool.affine_select(out=patchm[:, :], in_=patchm[:, :], compare_op=ALU.not_equal, fill=1.0,
                                            base=-(2 * NP * c + b), pattern=[[-2, NP]], channel_multiplier=1))
            step(pool.memset(ident[:, :], 0.0))
            step(pool.affine_select(out=ident[:, :], in_=ident[:, :], compare_op=ALU.not_equal, fill=1.0,
                                    base=0, pattern=[[-1, 128]], channel_multiplier=1))
            step(pool.tensor_copy(identb[:, :], ident[:, :]))
            step(pool.tensor_copy(ident16[:, :], ident[:, :]))
            step(pool.memset(ones[:, :], 1.0))
            step(pool.memset(mhalf[:, :], -0.5))
            step(pool.memset(band[:, :], 0.0))
            step(pool.affine_select(out=band[:, :], in_=band[:, :], compare_op=ALU.is_ge, fill=FAR,
                                    base=0, pattern=[[1, W]], channel_multiplier=-1))
            step(pool.affine_select(out=band[:, :], in_=band[:, :], compare_op=ALU.is_ge, fill=FAR,
                                    base=WIN - 1, pattern=[[-1, W]], channel_multiplier=1))
            step(pool.memset(causal[:, :], 1.0))
            step(pool.affine_select(out=causal[:, :], in_=causal[:, :], compare_op=ALU.is_ge, fill=0.0,
                                    base=0, pattern=[[1, P]], channel_multiplier=-1))
            step(pool.memset(brow[:, :], 0.0))
            step(pool.memset(headm[:, :], 1.0))
            step(pool.affine_select(out=headm[:, :], in_=headm[:, :], compare_op=ALU.is_ge, fill=0.0,
                                    base=0, pattern=[[-E, HC]], channel_multiplier=1))
            step(pool.affine_select(out=headm[:, :], in_=headm[:, :], compare_op=ALU.is_ge, fill=0.0,
                                    base=E - 1, pattern=[[E, HC]], channel_multiplier=-1))
            step(pool.memset(prob[:, :, :, :], 0.0))
            step(pool.memset(va[:, :, :, :], 1.0))
            step(pool.memset(vs[:, :, :, :], 1.0))
            step(pool.iota(iota8[:, :], pattern=[[1, NE]], base=0, channel_multiplier=0, allow_small_or_imprecise_dtypes=True))
            assert steps[0] == NSETUP, steps[0]

            def deviation(n, k):
                pool.wait_ge(var_ready.sem, var_ready.now(n, k + 1))
                hold(pool)
                _, var, r = moments_of(k)
                pool.tensor_scalar(r[:, :], var[:, :, 1], EPS, None, ALU.add).then_inc(eps_added.sem, 1)
                pool.wait_ge(eps_added.sem, eps_added.now(n, k + 1))
                pool.tensor_tensor(r[:, :], r[:, :], mhalf[:, :], ALU.pow).then_inc(rstd_ready.sem, 1)

            def gates(n):
                pool.wait_ge(top_ready.sem, top_ready.now(n, 1))
                b, k = place[("ye", NE - 1, 1)]
                pool.wait_ge(read[b].sem, read[b].before(n, k + 1))
                hold(pool)
                pool.tensor_copy(idxf[:, :, :], idx8[:, :, :]).then_inc(comb_ready.sem, 1)
                pool.wait_ge(comb_ready.sem, comb_ready.now(n, 1))
                hold(pool)
                for t in range(T):
                    pool.tensor_scalar(comb[:, t, :], iota8[:, :], idxf[:, t, 0:1], top8[:, t, 0:1], ALU.is_equal, ALU.mult)
                    ins = pool.tensor_scalar(comb2[:, t, :], iota8[:, :], idxf[:, t, 1:2], top8[:, t, 1:2], ALU.is_equal, ALU.mult)
                ins.then_inc(comb_ready.sem, 1)
                pool.wait_ge(comb_ready.sem, comb_ready.now(n, 2))
                pool.tensor_tensor(comb[:, :, :], comb[:, :, :], comb2[:, :, :], ALU.add).then_inc(comb_ready.sem, 1)

            def last_reader(k):
                return ("score", T * k + T - 1) if k < NU else ("ssm", (T * (k - NU) + T - 1) // 2)

            def copies(n, k):
                u = k % NU
                src = kT if k < NU else sqT
                if u % UC == 0:
                    if k < NU:
                        wait_read(pool, n, ("qk", 2 + u // UC))
                    else:
                        pool.wait_ge(elu_ready.sem, elu_ready.now(n, 1 + u // UC))
                if k < NX:
                    b, m = place[last_reader(k - NX + 2 * NU)]
                    pool.wait_ge(full[b].sem, full[b].before(n, m + 1))
                else:
                    wait_full(pool, n, last_reader(k - NX))
                hold(pool)
                for i in range(2):
                    h = (2 * u + i) % HC
                    ins = pool.tensor_scalar(hX[:, k % NX, i, :], src[:, u // UC, :], headm[:, h:h + 1], None, ALU.mult)
                ins.then_inc(hX_ready.sem, 1)

            def add_h0(n):
                pool.wait_ge(x16_ready.sem, x16_ready.now(n, 5))
                pool.tensor_tensor(hx[:, :, :], hx[:, :, :], h0[:, :, :], ALU.add).then_inc(h0_done.sem, 1)

            def scores(n, u):
                if 0 < u < NU - NX + 1:
                    copies(n, u + NX - 1)

            def first_copies(n, half):
                if half == 1:
                    for k in range(NX):
                        copies(n, k)

            def ssm_copies(n, k):
                for u in range(NU):
                    if (T * u + T - 1) // 2 == k - 1 and u + NX < NU:
                        copies(n, NU + u + NX)

            def attend(n, u):
                if u >= UC:
                    copies(n, NU + u - UC)

            nothing = lambda n, k=0: None
            def between(i, name, k):
                if (i, name) == (0, "x_T"):
                    pool.wait_ge(bias_lo, 1)

            run_schedule(dict(
                ssm_state=nothing, ssm=ssm_copies, reduce=nothing, so_T=nothing,
                so_out=lambda n: deviation(n, 2), ao_T=nothing, ao_split=nothing, norm2=nothing,
                patches=nothing, proj=nothing, sum_T=nothing, out=nothing, norm3=lambda n: deviation(n, 3),
                norm3b=nothing, x2_T=add_h0, mlp=nothing, tokens=nothing, norm4=lambda n: deviation(n, 4),
                norm0=lambda n: deviation(n, 0), z=nothing, norm1=lambda n: deviation(n, 1), z_T=nothing,
                gate=gates, norm1b=nothing, x_T=nothing, qk=first_copies, values=nothing, scores=scores,
                attend0=attend, attend1=nothing, attend2=nothing, moe=nothing), pool, between)

        @block.tensor
        def _(pe):
            mm = nc.tensor.matmul

            def open_tile(n, name):
                wait_free(pe, n, name)
                return at(name)

            def transpose_split(n, k):
                pe.wait_ge(x16_ready.sem, x16_ready.now(n, k + 1))
                o = open_tile(n, ("xT", k))[:, :].bitcast(fp16)
                for t in range(T):
                    for part in range(3):
                        ins = nc.tensor.transpose(o[:, part * L + t * P:part * L + (t + 1) * P],
                                                  x16[:, t, part * DA:(part + 1) * DA], ident16[0:P, 0:P])
                ins.then_inc(fullsem(("xT", k)), 1)

            def terms(a, b):
                return ((a(0, 128, 0), b(0, 128, 0)), (a(0, 128, 1), b(0, 128, 0)), (a(0, 128, 0), b(0, 128, 1)),
                        (a(0, 128, 2), b(0, 128, 2)), (a(0, DB, 2), b(0, DB, 3)))

            def token_major(o, k_xT, t, w, c, bias, start=True):
                parts = terms(lambda r0, r1, m: k_xT[r0:r1, m, t * P:(t + 1) * P], lambda r0, r1, m: w[r0:r1, m, c])
                mm(o, ones[:, :], brow[:, bias:bias + c.stop - c.start], start=start, stop=False, skip_group_check=True)
                for i, (a, b) in enumerate(parts):
                    ins = mm(o, a, b, start=False, stop=(i == 4), skip_group_check=True)
                return ins

            def feature_major(o, k_xT, w, c):
                parts = terms(lambda r0, r1, m: k_xT[r0:r1, m, :], lambda r0, r1, m: w[r0:r1, m, c])
                for i, (a, b) in enumerate(parts):
                    ins = mm(o, b, a, start=(i == 0), stop=(i == 4))
                return ins

            def linear(n, name, k, w, bias):
                wait_read(pe, n, ("xT", k))
                for pair, (t0, t1) in enumerate(PAIRS):
                    o = open_tile(n, (name, pair))
                    for t in range(t0, t1):
                        ins = token_major(o[0:P, (t - t0) * D:(t - t0 + 1) * D], xT[:, slot_xT(k)], t, w, slice(0, D), bias, t == t0)
                    ins.then_inc(fullsem((name, pair)), 1)

            def tokens(n):
                pe.wait_ge(patch_ready.sem, patch_ready.now(n, 3))
                for t, (a, b) in enumerate(((0, P), (P, IT))):
                    o = open_tile(n, ("tok", t))
                    for g in range(3):
                        ins = mm(o[0:b - a, 0:D], patch[:, g, :, :].rearrange("p i j -> p (i j)")[:, a:b],
                                 cwrep[:, g, :], start=(g == 0), stop=(g == 2))
                    ins.then_inc(fullsem(("tok", t)), 1)

            def qk(n, half):
                if half == 0:
                    wait_read(pe, n, ("xT", 0))
                for m in range(4 * half, 4 * half + 4):
                    o = open_tile(n, ("qk", m))
                    feature_major(o[0:DC, 0:L], xT[:, slot_xT(0)], wqkv[:, :, half], slice(m % 4 * DC, (m % 4 + 1) * DC))\
                        .then_inc(fullsem(("qk", m)), 1)

            def values(n):
                for t in range(T):
                    o = open_tile(n, ("v", t))
                    o = o[0:P, 0:2 * D].rearrange("p (a d) -> p a d", a=2)
                    mm(o, ones[:, :], brow[:, bv:bv + 2 * D].rearrange("p (a d) -> p a d", a=2), start=True, stop=False, skip_group_check=True)
                    parts = terms(lambda r0, r1, m: xT[r0:r1, slot_xT(0), m, t * P:(t + 1) * P],
                                  lambda r0, r1, m: wqkv[r0:r1, m, :, 2 * D:3 * D])
                    for i, (a, b) in enumerate(parts):
                        ins = mm(o, a, b, start=False, stop=(i == 4), skip_group_check=True)
                    ins.then_inc(fullsem(("v", t)), 1)

            def chunks(t):
                return (1,) if t == 0 else (0, 1)

            def scores(n, u):
                c = u // UC
                pe.wait_ge(hX_ready.sem, hX_ready.now(n, u + 1))
                if u % UC == 0:
                    wait_read(pe, n, ("qk", c))
                for t in range(T):
                    k = u * T + t
                    o = open_tile(n, ("score", k))
                    w = P if t == 0 else W
                    o = o[0:P, 0:2 * w].rearrange("p (i k) -> p i k", i=2)
                    mm(o, identb[0:P, 0:P], band[:, None, W - w:W].to_broadcast((P, 2, w)), start=True, stop=False)
                    mm(o, qT[:, c, t * P:(t + 1) * P], hX[:, u % NX, :, (t + 1) * P - w:(t + 1) * P],
                       start=False, stop=True).then_inc(fullsem(("score", k)), 1)

            def transposes(n, k):
                t = k % T
                wait_read(pe, n, ("score", k))
                o = open_tile(n, ("probT", k))[0:P, 0:4 * P].rearrange("p (i c q) -> p i c q", i=2, c=2)
                for i in range(2):
                    for c in chunks(t):
                        ins = nc.tensor.transpose(o[:, i, c, :], prob[:, k // T % 2, t, i, c * P:(c + 1) * P], ident[0:P, 0:P])
                ins.then_inc(fullsem(("probT", k)), 1)

            def head_sums(name):
                return at(name)[0:P, 0:T * HC * (E + 1)].rearrange("p (t h e) -> p t h e", t=T, h=HC)

            def weigh(n, k):
                u, t = UNITS[k]
                wait_read(pe, n, ("probT", k))
                o = head_sums(("ao", u // UC))
                for i in range(2):
                    for c in chunks(t):
                        ins = mm(o[:, t, (2 * u + i) % HC, :], probT[:, k % 2, i, c, :], va[:, t - 1 + c, 2 * u + i, :],
                                 start=(k % (UC * T) == 0 and i == 0 and c == 1), stop=(c == 1), skip_group_check=True)
                if k % (UC * T) == UC * T - 1:
                    ins.then_inc(fullsem(("ao", u // UC)), 1)

            def attend0(n, u):
                transposes(n, u * T)
                transposes(n, u * T + 1)

            def attend1(n, u):
                if u == 0:
                    for t in range(T):
                        wait_read(pe, n, ("v", t))
                if u % UC == 0:
                    open_tile(n, ("ao", u // UC))
                weigh(n, u * T)
                transposes(n, u * T + 2)
                weigh(n, u * T + 1)

            def attend2(n, u):
                weigh(n, u * T + 2)

            def ssm_state(n):
                pe.wait_ge(elu_ready.sem, elu_ready.now(n, 4))
                o = open_tile(n, ("skt",))[0:P, 0:2 * D].rearrange("p (t d) -> p t d", t=2)
                for t in range(2):
                    for c in range(2):
                        ins = nc.tensor.transpose(o[:, t, c * DC:(c + 1) * DC], skT[:, c, t * P:(t + 1) * P], ident[0:DC, 0:DC])
                ins.then_inc(fullsem(("skt",)), 1)
                wait_read(pe, n, ("skt",))
                o = open_tile(n, ("state",))[0:DC, 0:4 * HC * (E + 1)].rearrange("p (t c f) -> p t c f", t=2, c=2)
                for t in range(2):
                    for c in range(2):
                        for kt in range(t + 1):
                            ins = mm(o[:, t, c, :], sktok[:, kt, c * DC:(c + 1) * DC],
                                     vs[:, kt, c * HC:(c + 1) * HC, :].rearrange("p h e -> p (h e)"), start=(kt == 0), stop=(kt == t))
                ins.then_inc(fullsem(("state",)), 1)

            def ssm(n, k):
                if k == NSJ // 2 + 2:
                    ssm_sums(n, LATE)
                if k < NSJ:
                    o = open_tile(n, ("ssm", k))[0:P, 0:4 * P].rearrange("p (m i q) -> p m i q", m=2, i=2)
                    for m in range(2):
                        u, t = UNITS[2 * k + m]
                        if t == 0:
                            pe.wait_ge(hX_ready.sem, hX_ready.now(n, NU + u + 1))
                        ins = mm(o[:, m], skT[:, u // UC, t * P:(t + 1) * P], hX[:, (NU + u) % NX, :, t * P:(t + 1) * P],
                                 start=True, stop=True)
                    ins.then_inc(fullsem(("ssm", k)), 1)
                for unit in range(2 * (k - 1), 2 * k) if k else ():
                    if unit != LATE:
                        ssm_sums(n, unit)

            def ssm_sums(n, unit):
                u, t = UNITS[unit]
                c = u // UC
                o = head_sums(("so", c))
                wait_read(pe, n, ("ssm", unit // 2))
                if u % UC == 0 and t == 0:
                    if c == 0:
                        wait_read(pe, n, ("state",))
                    open_tile(n, ("so", c))
                    for s in range(2):
                        mm(o[:, s + 1], sqT[:, c, (s + 1) * P:(s + 2) * P], state[:, s, c, :, :].rearrange("p h e -> p (h e)"),
                           start=(s == 0), stop=False, skip_group_check=True)
                for i in range(2):
                    ins = mm(o[:, t, (2 * u + i) % HC, :], att[:, unit // 2 % NS, unit % 2, i, :], vs[:, t, 2 * u + i, :],
                             start=False, stop=True, skip_group_check=True)
                if u % UC == UC - 1 and t == T - 1:
                    ins.then_inc(fullsem(("so", c)), 1)

            def hidden(n, e, j):
                name = ("hid", e, j)
                o = open_tile(n, name)[:, 0:L]
                if e == NE:
                    ins = feature_major(o, xT[:, slot_xT(4)], wm1, slice(j * 128, (j + 1) * 128))
                else:
                    ins = feature_major(o, zT, w1[:, :, e], slice(j * 128, (j + 1) * 128))
                ins.then_inc(fullsem(name), 1)

            def second(n, e, j, k):
                if e == NE:
                    pe.wait_ge(blo_ready.sem, blo_ready.now(n, k + 1))
                    h16, w = bm16[:, k % NM], wm2[:, :, j * D:(j + 1) * D]
                else:
                    pe.wait_ge(lo_ready.sem, lo_ready.now(n, k + 1))
                    h16, w = hm16[:, k % NR], w2[:, :, e, j * D:(j + 1) * D]
                bias = bm2 if e == NE else bexp + e * D
                for pair, (t0, t1) in enumerate(PAIRS):
                    o = open_tile(n, ("ye", e, pair)) if j == 0 else at(("ye", e, pair))
                    for t in range(t0, t1):
                        if j == 0:
                            mm(o[0:P, (t - t0) * D:(t - t0 + 1) * D], ones[:, :], brow[:, bias:bias + D], start=(t == t0), stop=False,
                               skip_group_check=True)
                        for i, (a, b) in enumerate(((0, 0), (1, 0), (0, 1))):
                            ins = mm(o[0:P, (t - t0) * D:(t - t0 + 1) * D], h16[:, a, t * P:(t + 1) * P], w[:, b],
                                     start=False, stop=(j == NJ - 1 and i == 2), skip_group_check=True)
                    if j == NJ - 1:
                        ins.then_inc(fullsem(("ye", e, pair)), 1)

            def mlp(n, j):
                if j == 0:
                    wait_read(pe, n, ("xT", 4))
                    hidden(n, NE, 0)
                    return
                if j < NJ:
                    hidden(n, NE, j)
                if j >= LAGM:
                    second(n, NE, j - LAGM, j - LAGM)

            def moe(n, q):
                if q == 0:
                    wait_read(pe, n, ("xT", 5))
                if q < NE * NJ:
                    hidden(n, q // NJ, q % NJ)
                for k in seconds(q):
                    second(n, k // NJ, k % NJ, k)

            def gate_scores(n):
                wait_read(pe, n, ("xT", 5))
                o = open_tile(n, ("gate",))
                for t in range(T):
                    ins = token_major(o[0:P, t * NE:(t + 1) * NE], zT, t, wg, slice(0, NE), bgate, t == 0)
                ins.then_inc(fullsem(("gate",)), 1)

            nothing = lambda n, k=0: None
            pe.wait_ge(setup, NSETUP)
            pe.wait_ge(cw_loaded, 16 * C)
            pe.wait_ge(weights, 16 * NWEIGHTS)

            def between(i, name, k):
                if (i, name) == (0, "norm1b"):
                    pe.wait_ge(split_lo, NPB)
                if (i, name, k) == (0, "qk", 0):
                    pe.wait_ge(bias_lo, 1)
                if (i, name, k) == (1, "ssm", NSJ):
                    pe.wait_ge(split_lo, len(all_pieces))

            run_schedule(dict(
                ssm_state=ssm_state, ssm=ssm, reduce=nothing, so_T=lambda n: transpose_split(n, 2),
                so_out=lambda n: linear(n, "so2", 2, wsout, bsout), ao_T=lambda n: transpose_split(n, 1),
                ao_split=nothing, norm2=nothing, patches=nothing,
                proj=lambda n: linear(n, "sum", 1, wproj, bproj), sum_T=lambda n: transpose_split(n, 3),
                out=lambda n: linear(n, "out", 3, wout, bout), norm3=nothing, norm3b=nothing,
                x2_T=lambda n: transpose_split(n, 4), mlp=mlp, tokens=tokens, norm4=nothing, norm0=nothing,
                z=nothing, norm1=nothing, z_T=lambda n: transpose_split(n, 5), gate=gate_scores, norm1b=nothing,
                x_T=lambda n: transpose_split(n, 0), qk=qk, values=values, scores=scores, attend0=attend0,
                attend1=attend1, attend2=attend2, moe=moe), pe, between)

        @block.scalar
        def _(act):
            A = nc.scalar.activation

            def split_piece(k):
                _, n, (hi, _), _ = all_pieces[k]
                act.wait_ge(piece[k % NSLOT], piece_count[k])
                A(hi, stage[k % NSLOT][:, 0:n], ACT.Copy).then_inc(split_hi, 1)

            def evacuate(n, k):
                wait_full(act, n, ("xT", k))
                dst = zT[:, :, :] if k == 5 else xT[:, slot_xT(k)]
                A(dst.rearrange("p m l -> p (m l)"), at(("xT", k))[:, :].bitcast(fp16)[:, 0:3 * L], ACT.Copy).then_inc(readsem(("xT", k)), 1)

            def tokens(n):
                act.wait_ge(h0_done.sem, h0_done.before(n, 1))
                for t, m in ((0, P), (1, I1)):
                    wait_full(act, n, ("tok", t))
                    A(h0[0:m, t, :], at(("tok", t))[0:m, 0:D], ACT.Copy).then_inc(readsem(("tok", t)), 1)

            def qk(n, half):
                for m in range(4):
                    name = ("qk", 4 * half + m)
                    wait_full(act, n, name)
                    if half == 0:
                        dst = (qT, kT)[m // 2]
                        if m < 2:
                            A(dst[:, m, :], at(name)[0:DC, 0:L], ACT.Identity, scale=E ** -0.5, bias=bq4[:, m:m + 1]).then_inc(readsem(name), 1)
                        else:
                            A(dst[:, m - 2, :], at(name)[0:DC, 0:L], ACT.Identity, bias=bqk[:, m:m + 1]).then_inc(readsem(name), 1)
                    else:
                        act.wait_ge(elu_ready.sem, elu_ready.now(n, m - 1) if m >= 2 else elu_ready.before(n, 3 + m))
                        A(elue[:, m % 2, :], at(name)[0:DC, 0:L], ACT.Exp, bias=bqk[:, 4 + m:5 + m]).then_inc(elu_exp.sem, 1)

            def values(n):
                A(unused[:, :], mhalf[0:1, 0:1], ACT.Exp)
                for t in range(T):
                    name = ("v", t)
                    wait_full(act, n, name)
                    o = at(name)[0:P, 0:2 * D].rearrange("p (a h e) -> p a h e", a=2, h=H)
                    A(va[:, t, :, 0:E], o[:, 0, :, :], ACT.Copy)
                    A(vs[:, t, :, 0:E], o[:, 1, :, :], ACT.Copy).then_inc(readsem(name), 1)

            def scores(n, u):
                for t in range(T):
                    k = u * T + t
                    w = P if t == 0 else W
                    act.wait_ge(nmax_ready.sem, nmax_ready.now(n, k + 1))
                    o = at(("score", k))[0:P, 0:2 * w].rearrange("p (i k) -> p i k", i=2)
                    for i in range(2):
                        ins = A(prob[:, u % 2, t, i, 2 * P - w:2 * P], o[:, i, :], ACT.Exp, bias=nmax[:, u % 2, t, i:i + 1])
                    ins.then_inc(readsem(("score", k)), 1)

            def ssm_state(n):
                wait_full(act, n, ("skt",))
                A(sktok[:, :, :].rearrange("p t d -> p (t d)"), at(("skt",))[0:P, 0:2 * D], ACT.Copy).then_inc(readsem(("skt",)), 1)

            def hidden(n, e, j, dst, dst16):
                name = ("hid", e, j)
                wait_full(act, n, name)
                A(dst, at(name)[:, 0:L], ACT.Gelu, bias=bh[:, e, j:j + 1])
                A(dst16, at(name)[:, 0:L], ACT.Gelu, bias=bh[:, e, j:j + 1]).then_inc(readsem(name), 1)

            def mlp(n, j):
                if j < NJ:
                    hidden(n, NE, j, bm[:, j % NM, :], bm16[:, j % NM, 0, :])

            def moe(n, q):
                if q < NE * NJ:
                    hidden(n, q // NJ, q % NJ, hm[:, q % NR, :], hm16[:, q % NR, 0, :])

            nothing = lambda n, k=0: None
            load = lambda dst, src: act.dma_start(dst, src).then_inc(weights, 16)
            row = lambda b, r=1: b.rearrange("(o d) -> o d", o=1).to_broadcast((r, b.shape[0]))
            for r in (0, 32):
                for o, b in ((bv, qkv_b[2 * D:3 * D]), (bv + D, sqkv_b[2 * D:3 * D]), (bproj, proj_b), (bsout, sout_b),
                             (bout, out_b), (bm2, mlp_b2)):
                    load(brow32[r:r + 1, o:o + b.shape[0]], row(b))
                load(bg32[r:r + 1, :], row(bg))
                load(bexp32[r:r + 1, :], row(b2.rearrange("e d -> (e d)")))
            for k, (g_, b_) in enumerate(((ln1_g, ln1_b), (sln_g, sln_b), (lnm_g, lnm_b))):
                load(lnw[:, k, 0, :], row(g_, P))
                load(lnw[:, k, 1, :], row(b_, P))
            with nc.allow_non_contiguous_dma(reason="biases to columns, once"):
                for k, b in enumerate((qkv_b, sqkv_b)):
                    load(bqk[:, 4 * k:4 * k + 4], b[0:2 * D].rearrange("(m p) -> p m", p=DC))
                load(bh[:, 0:NE, :], b1.rearrange("e (j p) -> p e j", p=128))
                load(bh[:, NE, :], mlp_b1.rearrange("(j p) -> p j", p=128))
            act.wait_ge(setup, NSETUP)
            act.wait_ge(weights, 16 * NWEIGHTS)
            split_pieces = [0]

            def between(i, name, k):
                if (i, name) == (0, "x_T"):
                    act.wait_ge(bias_cols, 1)
                if (i, name) == (0, "values"):
                    act.wait_ge(bias_lo, 1)
                for _ in range(pieces_after(i, name)):
                    if split_pieces[0] < len(all_pieces):
                        split_piece(split_pieces[0])
                        split_pieces[0] += 1

            run_schedule(dict(
                ssm_state=ssm_state, ssm=nothing, reduce=nothing, so_T=lambda n: evacuate(n, 2), so_out=nothing,
                ao_T=lambda n: evacuate(n, 1), ao_split=nothing, norm2=nothing, patches=nothing, proj=nothing,
                sum_T=lambda n: evacuate(n, 3), out=nothing, norm3=nothing, norm3b=nothing,
                x2_T=lambda n: evacuate(n, 4), mlp=mlp, tokens=tokens, norm4=nothing, norm0=nothing, z=nothing,
                norm1=nothing, z_T=lambda n: evacuate(n, 5), gate=nothing, norm1b=nothing,
                x_T=lambda n: evacuate(n, 0), qk=qk, values=values, scores=scores, attend0=nothing,
                attend1=nothing, attend2=nothing, moe=moe), act, between)

        @block.vector
        def _(dve):
            V = nc.vector
            links = {}

            def split_piece(k):
                kind, n, (hi, lo), _ = all_pieces[k]
                dve.wait_ge(split_hi, k + 1)
                r = slice(0, DB) if kind == "rest" else slice(0, 128)
                V.tensor_tensor(lo, stage[k % NSLOT][r, 0:n], hi[r], ALU.subtract).then_inc(split_lo, 1)

            def link(n, part, ins):
                links[part] += 1
                ins.then_inc(part.sem, 1)
                dve.wait_ge(part.sem, part.now(n, links[part]))

            def linked(part):
                assert links[part] == part.per, (part.sem, links[part])

            def part_of_norm(k):
                return (first, first, second_part, second_part, gating)[k]

            def tile_of(name, pair):
                return (*name, pair) if isinstance(name, tuple) else (name, pair)

            def tok(name, pair):
                t0, t1 = PAIRS[pair]
                return at(tile_of(name, pair))[0:P, 0:(t1 - t0) * D].rearrange("p (t d) -> p t d", d=D)

            def moments(n, k, src):
                st, m, _ = moments_of(k)
                for t in range(T):
                    ins = V.bn_stats(st[:, t, :], src(t))
                link(n, part_of_norm(k), ins)
                hold(dve)
                for t in range(T):
                    ins = V.bn_aggr(m[:, t, :], st[:, t, :])
                ins.then_inc(var_ready.sem, 1)

            def scale(n, k, src, dst):
                _, m, r = moments_of(k)
                dve.wait_ge(rstd_ready.sem, rstd_ready.now(n, k + 1))
                for t in range(T):
                    ins = V.tensor_scalar(dst[:, t, :], src(t), m[:, t, 0:1], r[:, t:t + 1], ALU.subtract, ALU.mult)
                return ins

            def centre(n, k, src, dst):
                dve.wait_ge(var_ready.sem, var_ready.now(n, k + 1))
                return [V.scalar_tensor_tensor(dst[:, t, :], src(t), mv[:, t, 0:1], lnw[:, k - 1, 0, :], ALU.subtract, ALU.mult) for t in range(T)]

            def affine(n, k, buf):
                dve.wait_ge(rstd_ready.sem, rstd_ready.now(n, k + 1))
                for t in range(T):
                    ins = V.scalar_tensor_tensor(buf[:, t, :], buf[:, t, :], rstd[:, t:t + 1], lnw[:, k - 1, 1, :], ALU.mult, ALU.add)
                return ins

            def split(n, k, src):
                if k >= 1:
                    wait_full(dve, n, ("xT", k - 1))
                d = x16
                V.tensor_copy(d[:, :, 0:DA], src[:, :, 0:DA])
                link(n, (first, second_part, second_part, second_part, second_part, gating)[k], V.tensor_copy(d[:, :, 2 * DA:2 * DA + DB], src[:, :, DA:D]))
                V.tensor_tensor(d[:, :, DA:2 * DA], src[:, :, 0:DA], d[:, :, 0:DA], ALU.subtract)
                V.tensor_tensor(d[:, :, 2 * DA + DB:2 * D], src[:, :, DA:D], d[:, :, 2 * DA:2 * DA + DB], ALU.subtract)\
                    .then_inc(x16_ready.sem, 1)

            def of(buf):
                return lambda t: buf[:, t, :]

            def reduce(n, h):
                dve.wait_ge(x_loaded[h % 2].sem, x_loaded[h % 2].now(n, 16 * (h // 2 + 1)))
                V.tensor_reduce(pooled[:, h, :], xin[:, h % 2, :].rearrange("p (r j w) -> p j r w", j=NP, w=KP),
                                axis=AX.XY, op=ALU.add).then_inc(x_read.sem, 1)

            def patches(n):
                links[first] = 0
                dve.wait_ge(x_read.sem, x_read.now(n, 6))
                link(n, first, V.tensor_tensor(pooled[:, 0:3, :], pooled[:, 0:3, :], pooled[:, 3:6, :], ALU.add))
                for g in range(3):
                    V.tensor_tensor(patch[:, g, :, :], pooled[:, g, None, :].to_broadcast((PX, NP, NP)),
                                    patchm[:, :, None].to_broadcast((PX, NP, NP)), ALU.mult).then_inc(patch_ready.sem, 1)

            def norm0(n):
                for t in range(2):
                    wait_read(dve, n, ("tok", t))
                dve.wait_ge(txt_loaded.sem, txt_loaded.now(n, 32))
                moments(n, 0, of(h0))

            def norm1(n):
                link(n, first, scale(n, 0, of(h0), y))
                moments(n, 1, of(y))
                link(n, first, centre(n, 1, of(y), xn)[-1])

            def norm1b(n):
                link(n, first, affine(n, 1, xn))
                split(n, 0, xn)

            def qk(n, half):
                for m in range(4 * half):
                    name = ("qk", 4 + m)
                    dve.wait_ge(elu_exp.sem, elu_exp.now(n, m + 1))
                    V.tensor_scalar(elur[:, m % 2, :], at(name)[0:DC, 0:L], bneg[:, m:m + 1], bpos[:, m:m + 1],
                                    ALU.max, ALU.add).then_inc(readsem(name), 1)
                    wait_read(dve, n, name)
                    if m == 0:
                        dve.wait_ge(hX_ready.sem, hX_ready.before(n, 2 * NU))
                    V.scalar_tensor_tensor((sqT, skT)[m // 2][:, m % 2, :], elue[:, m % 2, :], 1.0, elur[:, m % 2, :],
                                           ALU.min, ALU.add).then_inc(elu_ready.sem, 1)

            def scores(n, u):
                for t in range(T):
                    k = u * T + t
                    w = P if t == 0 else W
                    wait_full(dve, n, ("score", k))
                    V.tensor_reduce(nmax[:, u % 2, t, :], at(("score", k))[0:P, 0:2 * w].rearrange("p (i k) -> p i k", i=2),
                                    axis=AX.X, op=ALU.max, negate=True).then_inc(nmax_ready.sem, 1)

            def weights_T(n, k):
                if k == 0:
                    dve.wait_ge(elu_ready.sem, elu_ready.now(n, 4))
                wait_full(dve, n, ("probT", k))
                c0 = 1 if k % T == 0 else 0
                o = at(("probT", k))[0:P, 0:4 * P].rearrange("p (i c q) -> p i c q", i=2, c=2)
                V.tensor_copy(probT[:, k % 2, :, c0:2, :], o[:, :, c0:2, :]).then_inc(readsem(("probT", k)), 1)

            def attend0(n, u):
                weights_T(n, u * T)
                weights_T(n, u * T + 1)

            def attend1(n, u):
                weights_T(n, u * T + 2)

            def attend2(n, u):
                if u % UC == UC - 1:
                    normalise(n, ("ao", u // UC), 0.0, ao)
                if u == NU - 1:
                    linked(first)

            def normalise(n, name, eps, dst):
                c = name[1]
                wait_full(dve, n, name)
                o = at(name)[0:P, 0:T * HC * (E + 1)].rearrange("p (t h e) -> p t h e", t=T, h=HC)
                part = first if name[0] == "ao" else second_part
                link(n, part, V.tensor_scalar(den[:, :, :], o[:, :, :, E], eps, None, ALU.add))
                link(n, part, V.reciprocal(den[:, :, :], den[:, :, :]))
                V.tensor_tensor(dst[:, :, c * HC:(c + 1) * HC, :], o[:, :, :, 0:E], den[:, :, :, None].to_broadcast((P, T, HC, E)),
                                ALU.mult).then_inc(readsem(name), 1)

            def ssm_state(n):
                links[second_part] = 0
                wait_full(dve, n, ("state",))
                V.tensor_tensor(state[:, :, :, :, :].rearrange("p t c h e -> p (t c) h e"),
                                at(("state",))[0:DC, 0:4 * HC * (E + 1)].rearrange("p (m h e) -> p m h e", m=4, h=HC),
                                headm[:, None, :, None].to_broadcast((DC, 4, HC, E + 1)), ALU.mult).then_inc(readsem(("state",)), 1)

            def ssm(n, k):
                if k < NSJ:
                    wait_full(dve, n, ("ssm", k))
                    V.tensor_tensor(att[:, k % NS].rearrange("p m i q -> p (m i) q"), at(("ssm", k))[0:P, 0:4 * P].rearrange("p (m q) -> p m q", m=4),
                                    causal[:, None, :].to_broadcast((P, 4, P)), ALU.mult).then_inc(readsem(("ssm", k)), 1)
                if k in (NSJ // 2 + 1, NSJ):
                    normalise(n, ("so", k // NSJ), 1e-4 * E ** 0.5, so)

            flat = lambda b: b[:, :, :, :].rearrange("p t h e -> p t (h e)")

            def so_T(n):
                wait_read(dve, n, ("so", 1))
                split(n, 2, flat(so))

            def ao_split(n):
                split(n, 1, flat(ao))

            def so_tile(t):
                return tok("so2", t // 2)[:, t % 2, :]

            def so_out(n):
                for pair in range(2):
                    wait_full(dve, n, ("so2", pair))
                moments(n, 2, so_tile)
                _, t1, t2 = centre(n, 2, so_tile, so2)
                t1.then_inc(readsem(("so2", 0)), 1)
                t2.then_inc(readsem(("so2", 1)), 1)

            def norm2(n):
                wait_read(dve, n, ("so2", 1))
                link(n, second_part, affine(n, 2, so2))

            def add_pairs(n, name, dst, other):
                for pair, (t0, t1) in enumerate(PAIRS):
                    tile = tile_of(name, pair)
                    wait_full(dve, n, tile)
                    V.tensor_tensor(dst[:, t0:t1, :], tok(name, pair), other[:, t0:t1, :], ALU.add).then_inc(readsem(tile), 1)
                for pair in range(2):
                    wait_read(dve, n, tile_of(name, pair))

            def proj(n):
                add_pairs(n, "sum", so2, so2)
                split(n, 3, so2)

            def out_(n):
                add_pairs(n, "out", hx, y)
                moments(n, 3, of(hx))
                link(n, second_part, centre(n, 3, of(hx), xn)[-1])

            def norm3(n):
                link(n, second_part, affine(n, 3, xn))

            def norm3b(n):
                split(n, 4, xn)

            def mlp(n, j):
                if j < NJ:
                    wait_read(dve, n, ("hid", NE, j))
                    V.tensor_tensor(bm16[:, j % NM, 1, :], bm[:, j % NM, :], bm16[:, j % NM, 0, :], ALU.subtract).then_inc(blo_ready.sem, 1)
                if j == NJ + LAGM - 1:
                    dve.wait_ge(h0_done.sem, h0_done.now(n, 1))
                    add_pairs(n, ("ye", NE), hx, hx)
                    linked(second_part)

            def norm4(n):
                links[gating] = 0
                moments(n, 4, of(hx))

            def z(n):
                link(n, gating, scale(n, 4, of(hx), xn))
                split(n, 5, xn)

            def gate_scores(n):
                wait_full(dve, n, ("gate",))
                V.tensor_copy(gate[:, :, :], at(("gate",))[0:P, 0:T * NE].rearrange("p (t e) -> p t e", t=T)).then_inc(readsem(("gate",)), 1)
                wait_read(dve, n, ("gate",))
                hold(dve)
                for t in range(T):
                    ins = V.max(top8[:, t, :], gate[:, t, :])
                link(n, gating, ins)
                hold(dve)
                for t in range(T):
                    ins = V.max_index(idx8[:, t, :], top8[:, t, :], gate[:, t, :])
                ins.then_inc(top_ready.sem, 1)
                linked(gating)

            def moe(n, q):
                if 1 <= q <= NE * NJ:
                    k = q - 1
                    wait_read(dve, n, ("hid", k // NJ, k % NJ))
                    V.tensor_tensor(hm16[:, k % NR, 1, :], hm[:, k % NR, :], hm16[:, k % NR, 0, :], ALU.subtract).then_inc(lo_ready.sem, 1)
                for k in seconds(q):
                    if k % NJ == NJ - 1:
                        add_expert(n, k // NJ)

            def add_expert(n, e):
                if e == 0:
                    dve.wait_ge(comb_ready.sem, comb_ready.now(n, 3))
                    dve.wait_ge(stored.sem, stored.before(n, 16))
                for pair, (t0, t1) in enumerate(PAIRS):
                    name = ("ye", e, pair)
                    wait_full(dve, n, name)
                    if e:
                        wait_read(dve, n, ("ye", e - 1, pair))
                    for t in range(t0, t1):
                        ins = V.scalar_tensor_tensor(hres[:, t, :], at(name)[0:P, (t - t0) * D:(t - t0 + 1) * D], comb[:, t, e:e + 1],
                                                     (hres if e else hx)[:, t, :], ALU.mult, ALU.add)
                    ins.then_inc(readsem(name), 1)

            def biases():
                V.tensor_scalar(bq4[:, :], bqk[:, 0:2], E ** -0.5, None, ALU.mult)
                V.tensor_scalar(bneg[:, :], bqk[:, 4:8], -1.0, None, ALU.mult)
                V.tensor_scalar(bpos[:, :], bqk[:, 4:8], 1e-4, None, ALU.add).then_inc(bias_cols, 1)
                parts = ((brow32, slice(0, bgate)), (bg32, slice(bgate, bexp)), (bexp32, slice(bexp, NBR)))
                for b32, c in parts:
                    V.tensor_copy(brow[0:1, c], b32[0:1, :])
                    V.tensor_copy(brow[32:33, c], b32[32:33, :]).then_inc(bias_hi, 1)
                dve.wait_ge(bias_hi, len(parts))
                for b32, c in parts:
                    ins = V.tensor_tensor(brow[32:33, c], b32[32:33, :], brow[32:33, c], ALU.subtract)
                ins.then_inc(bias_lo, 1)

            nothing = lambda n, k=0: None
            dve.wait_ge(setup, NSETUP)
            split_pieces = [0]

            def between(i, name, k):
                if (i, name) == (0, "norm0"):
                    dve.wait_ge(weights, 16 * NWEIGHTS)
                if (i, name) == (0, "norm1b"):
                    biases()
                for _ in range(pieces_after(i, name)):
                    if split_pieces[0] < len(all_pieces):
                        split_piece(split_pieces[0])
                        split_pieces[0] += 1

            run_schedule(dict(
                ssm_state=ssm_state, ssm=ssm, reduce=reduce, so_T=so_T, so_out=so_out, norm2=norm2,
                ao_split=ao_split, ao_T=nothing, patches=patches, proj=proj, sum_T=nothing, out=out_,
                norm3=norm3, norm3b=norm3b, x2_T=nothing, mlp=mlp, tokens=nothing, norm4=norm4, norm0=norm0,
                z=z, norm1=norm1, z_T=nothing, gate=gate_scores, norm1b=norm1b, x_T=nothing, qk=qk,
                values=nothing, scores=scores, attend0=attend0, attend1=attend1, attend2=attend2, moe=moe), dve, between)


_INS = ['x', 'txt', 'L0_tok_channel_weights', 'L0_attn_ln1_g', 'L0_attn_ln1_b', 'L0_attn_attn_qkv_w', 'L0_attn_attn_qkv_b',
        'L0_attn_attn_proj_w', 'L0_attn_attn_proj_b', 'L0_attn_ssm_qkv_w', 'L0_attn_ssm_qkv_b', 'L0_attn_ssm_out_w',
        'L0_attn_ssm_out_b', 'L0_attn_ssm_ln_g', 'L0_attn_ssm_ln_b', 'L0_attn_out_w', 'L0_attn_out_b', 'L0_attn_mlp_w1',
        'L0_attn_mlp_b1', 'L0_attn_mlp_w2', 'L0_attn_mlp_b2', 'L0_attn_lnm_g', 'L0_attn_lnm_b',
        'L0_ffn_Wg', 'L0_ffn_bg', 'L0_ffn_W1', 'L0_ffn_b1', 'L0_ffn_W2', 'L0_ffn_b2']
_OUTS = [((16, 324, 192), 'float32')]


def kernel(**inputs):
    import numpy as _np
    import concourse.bacc as _bacc
    from concourse import mybir as _mybir
    from concourse.bass_utils import run_bass_kernel_spmd as _run

    nc = _bacc.Bacc("TRN2", target_bir_lowering=False, num_devices=1)
    arrays, args = {}, []
    for name in _INS:
        a = _np.ascontiguousarray(inputs[name])
        arrays[f"in_{name}_dram"] = a
        args.append(nc.dram_tensor(f"in_{name}_dram", a.shape, _mybir.dt.from_np(a.dtype), kind="ExternalInput").ap())
    for i, (shape, dtype) in enumerate(_OUTS):
        dt = _mybir.dt.from_np(_np.dtype(dtype))
        args.append(nc.dram_tensor(f"out_{i}_dram", shape, dt, kind="ExternalOutput").ap())
    early_fusion_moe_kernel(nc, *args)
    r = _run(nc, [arrays], core_ids=[0])
    return r.results[0]["out_0_dram"]
```
